# Optimizing a Trainium2 kernel written in Bass

```python
import numpy as np
import jax
import jax.numpy as jnp

def _softmax(x, axis=-1):
    return jax.nn.softmax(x, axis=axis)

def _gelu(x):
    return jax.nn.gelu(x, approximate=True)

def _silu(x):
    return jax.nn.silu(x)

def _sigmoid(x):
    return jax.nn.sigmoid(x)

def _layernorm(x, axis=-1, eps=1e-05):
    m = jnp.mean(x, axis=axis, keepdims=True)
    v = jnp.var(x, axis=axis, keepdims=True)
    return (x - m) / jnp.sqrt(v + eps)

def _scatter_add(tgt, idx, src, axis=0):
    return tgt.at[idx].add(src)

def _segment_sum(src, seg, n):
    return jax.ops.segment_sum(src, seg, n)
kernel_name = 'mk_gnn_preln_d4_gnn_r16_f25bb6'

def setup_inputs(seed: int=0):
    np.random.seed(seed)
    _w = jnp.asarray

    def _rec_inputs():
        import jax
        import jax.numpy as jnp
        _gk = jax.random.key(seed)
        x = -0.0008691 + 1 * jax.random.normal(jax.random.fold_in(_gk, 1), (6250, 128), jnp.float32)
        src = jax.random.randint(jax.random.fold_in(_gk, 2), (200000,), 0, 6250, jnp.int32)
        dst = jax.random.randint(jax.random.fold_in(_gk, 3), (200000,), 0, 6250, jnp.int32)
        _o = jnp.argsort(dst, stable=True)
        src = src[_o]
        dst = dst[_o]
        edge_type_9 = jax.random.randint(jax.random.fold_in(_gk, 12), (200000,), 0, 9, jnp.int32)
        edge_weight1 = jax.random.uniform(jax.random.fold_in(_gk, 13), (200000, 1), jnp.float32, 0.0, 1)
        return (x, src, dst, edge_type_9, edge_weight1)
    x, src, dst, edge_type_9, edge_weight1 = _rec_inputs()

    def _L0_gnn_setup():
        import jax, jax.numpy as jnp
        import numpy as np
        N_NODES = 625
        N_EDGES = 40000
        D_FEAT = 128
        key = jax.random.key(seed)
        k1, k2 = jax.random.split(key)
        x = jax.random.normal(k1, (N_NODES, D_FEAT), dtype=jnp.float32)
        edge_index = jax.random.randint(k2, (2, N_EDGES), 0, N_NODES, dtype=jnp.int32)
        return {'x': x, 'edge_index': edge_index}
    _L0_gnn_all = _L0_gnn_setup()
    _L0_gnn_in = {k: v for k, v in _L0_gnn_all.items() if k in ()}
    del _L0_gnn_all

    def _L1_gnn_setup():
        import jax, jax.numpy as jnp
        import numpy as np
        N_NODES = 6250
        N_EDGES = 625000
        D_FEAT = 128
        OUT_DIM = 128
        key = jax.random.key(seed)
        k1, k2, k3, k4 = jax.random.split(key, 4)
        feature = jax.random.normal(k1, (N_NODES, D_FEAT), dtype=jnp.float32)
        relation_weight = jax.random.uniform(k2, (N_EDGES, 1), dtype=jnp.float32)
        relation_indices = jax.random.randint(k3, (2, N_EDGES), 0, N_NODES, dtype=jnp.int32)
        W = jax.random.normal(k4, (2 * D_FEAT, OUT_DIM), dtype=jnp.float32) * 0.05
        b = jnp.zeros((OUT_DIM,), dtype=jnp.float32)
        return {'feature': feature, 'relation_weight': relation_weight, 'W': W, 'b': b, 'relation_indices': relation_indices}
    _L1_gnn_all = _L1_gnn_setup()
    _L1_gnn_in = {k: v for k, v in _L1_gnn_all.items() if k in ('W', 'b')}
    del _L1_gnn_all

    def _L2_gnn_setup():
        import jax, jax.numpy as jnp
        import numpy as np
        NUM_EDGE_TYPES = 8
        HIDDEN = 128
        N_NODES = 3125
        N_EDGES = 37500

        def _gru_cell(x, h, W_ih, W_hh, b_ih, b_hh):
            H = h.shape[-1]
            gi = x @ W_ih.T + b_ih
            gh = h @ W_hh.T + b_hh
            i_r, i_z, i_n = (gi[:, :H], gi[:, H:2 * H], gi[:, 2 * H:])
            h_r, h_z, h_n = (gh[:, :H], gh[:, H:2 * H], gh[:, 2 * H:])
            r = jax.nn.sigmoid(i_r + h_r)
            z = jax.nn.sigmoid(i_z + h_z)
            n = jnp.tanh(i_n + r * h_n)
            return (1.0 - z) * n + z * h
        key = jax.random.key(seed)
        ks = jax.random.split(key, 10)
        H = HIDDEN
        h = jax.random.normal(ks[0], (N_NODES, H), dtype=jnp.float32)
        edge_index = jax.random.randint(ks[1], (2, N_EDGES), 0, N_NODES, dtype=jnp.int32)
        edge_type = jax.random.randint(ks[2], (N_EDGES,), 0, NUM_EDGE_TYPES + 1, dtype=jnp.int32)
        s = 1.0 / np.sqrt(H)
        W_msg = jax.random.uniform(ks[3], (H, H), jnp.float32, -s, s)
        b_msg = jax.random.uniform(ks[4], (H,), jnp.float32, -s, s)
        edge_embed = jax.random.normal(ks[5], (NUM_EDGE_TYPES + 1, H), dtype=jnp.float32)
        W_ih = jax.random.uniform(ks[6], (3 * H, H), jnp.float32, -s, s)
        W_hh = jax.random.uniform(ks[7], (3 * H, H), jnp.float32, -s, s)
        b_ih = jax.random.uniform(ks[8], (3 * H,), jnp.float32, -s, s)
        b_hh = jax.random.uniform(ks[9], (3 * H,), jnp.float32, -s, s)
        return {'h': h, 'edge_index': edge_index, 'edge_type': edge_type, 'num_nodes': N_NODES, 'W_msg': W_msg, 'b_msg': b_msg, 'edge_embed': edge_embed, 'W_ih': W_ih, 'W_hh': W_hh, 'b_ih': b_ih, 'b_hh': b_hh}
    _L2_gnn_all = _L2_gnn_setup()
    _L2_gnn_in = {k: v for k, v in _L2_gnn_all.items() if k in ('W_msg', 'b_msg', 'edge_embed', 'W_ih', 'W_hh', 'b_ih', 'b_hh')}
    del _L2_gnn_all

    def _L3_gnn_setup():
        import jax, jax.numpy as jnp
        import numpy as np
        N_NODES = 6250
        N_EDGES = 100000
        IN_CH = 128
        OUT_CH = 32
        HEADS = 4
        NEG_SLOPE = 0.2
        key = jax.random.key(seed)
        k1, k2, k3, k4 = jax.random.split(key, 4)
        x = jax.random.normal(k1, (N_NODES, IN_CH), dtype=jnp.float32)
        weight = jax.random.normal(k2, (IN_CH, HEADS * OUT_CH), dtype=jnp.float32) * 0.1
        att = jax.random.normal(k3, (1, HEADS, 2 * OUT_CH), dtype=jnp.float32) * 0.1
        edge_index = jax.random.randint(k4, (2, N_EDGES), 0, N_NODES, dtype=jnp.int64)
        return {'x': x, 'weight': weight, 'att': att, 'edge_index': edge_index}
    _L3_gnn_all = _L3_gnn_setup()
    _L3_gnn_in = {k: v for k, v in _L3_gnn_all.items() if k in ('weight', 'att')}
    del _L3_gnn_all
    return {'x': x, 'src': src, 'dst': dst, 'edge_type_9': edge_type_9, 'edge_weight1': edge_weight1, 'L1_gnn_W': _L1_gnn_in['W'], 'L1_gnn_b': _L1_gnn_in['b'], 'L2_gnn_W_msg': _L2_gnn_in['W_msg'], 'L2_gnn_b_msg': _L2_gnn_in['b_msg'], 'L2_gnn_edge_embed': _L2_gnn_in['edge_embed'], 'L2_gnn_W_ih': _L2_gnn_in['W_ih'], 'L2_gnn_W_hh': _L2_gnn_in['W_hh'], 'L2_gnn_b_ih': _L2_gnn_in['b_ih'], 'L2_gnn_b_hh': _L2_gnn_in['b_hh'], 'L3_gnn_weight': _L3_gnn_in['weight'], 'L3_gnn_att': _L3_gnn_in['att']}

def reference(x, src, dst, edge_type_9, edge_weight1, L1_gnn_W, L1_gnn_b, L2_gnn_W_msg, L2_gnn_b_msg, L2_gnn_edge_embed, L2_gnn_W_ih, L2_gnn_W_hh, L2_gnn_b_ih, L2_gnn_b_hh, L3_gnn_weight, L3_gnn_att):
    import jax
    import jax.numpy as jnp

    def _L0_gnn_ref(x, edge_index):
        import jax, jax.numpy as jnp
        import numpy as np
        N_NODES = 625
        N_EDGES = 40000
        D_FEAT = 128
        src = edge_index[0]
        dst = edge_index[1]
        msg = jnp.take(x, src, axis=0)
        out = jax.ops.segment_sum(msg, dst, num_segments=x.shape[0])
        return out

    def _L1_gnn_ref(feature, relation_weight, W, b, relation_indices):
        import jax, jax.numpy as jnp
        import numpy as np
        N_NODES = 6250
        N_EDGES = 625000
        D_FEAT = 128
        OUT_DIM = 128
        dst = relation_indices[0]
        src = relation_indices[1]
        n = feature.shape[0]
        feat_n = feature[src] * relation_weight
        seg_sum = jax.ops.segment_sum(feat_n, dst, num_segments=n)
        seg_cnt = jax.ops.segment_sum(jnp.ones((src.shape[0], 1), feat_n.dtype), dst, num_segments=n)
        neigh_mean = seg_sum / jnp.maximum(seg_cnt, 1.0)
        h = jnp.concatenate([feature, neigh_mean], axis=-1)
        return h @ W + b

    def _L2_gnn_ref(h, edge_index, edge_type, num_nodes, W_msg, b_msg, edge_embed, W_ih, W_hh, b_ih, b_hh):
        import jax, jax.numpy as jnp
        import numpy as np
        NUM_EDGE_TYPES = 8
        HIDDEN = 128
        N_NODES = 3125
        N_EDGES = 37500

        def _gru_cell(x, h, W_ih, W_hh, b_ih, b_hh):
            H = h.shape[-1]
            gi = x @ W_ih.T + b_ih
            gh = h @ W_hh.T + b_hh
            i_r, i_z, i_n = (gi[:, :H], gi[:, H:2 * H], gi[:, 2 * H:])
            h_r, h_z, h_n = (gh[:, :H], gh[:, H:2 * H], gh[:, 2 * H:])
            r = jax.nn.sigmoid(i_r + h_r)
            z = jax.nn.sigmoid(i_z + h_z)
            n = jnp.tanh(i_n + r * h_n)
            return (1.0 - z) * n + z * h
        src = edge_index[0]
        dst = edge_index[1]
        src_h = h[src] @ W_msg.T + b_msg
        emb = edge_embed[jnp.clip(edge_type, 0, NUM_EDGE_TYPES)]
        msg = src_h + emb
        messages = jax.ops.segment_sum(msg, dst, num_segments=num_nodes)
        h_new = _gru_cell(messages, h[:num_nodes], W_ih, W_hh, b_ih, b_hh)
        result = jnp.zeros_like(h).at[:num_nodes].set(h_new)
        return result

    def _L3_gnn_ref(x, weight, att, edge_index):
        import jax, jax.numpy as jnp
        import numpy as np
        N_NODES = 6250
        N_EDGES = 100000
        IN_CH = 128
        OUT_CH = 32
        HEADS = 4
        NEG_SLOPE = 0.2
        num_nodes = x.shape[0]
        h = jnp.matmul(x, weight).reshape(num_nodes, HEADS, OUT_CH)
        row, col = (edge_index[0], edge_index[1])
        x_i = h[row]
        x_j = h[col]
        a_i = att[0, :, :OUT_CH]
        a_j = att[0, :, OUT_CH:]
        alpha = jnp.einsum('ehc,hc->eh', x_i, a_i) + jnp.einsum('ehc,hc->eh', x_j, a_j)
        alpha = jnp.where(alpha >= 0, alpha, NEG_SLOPE * alpha)
        amax = jax.ops.segment_max(alpha, col, num_segments=num_nodes)
        amax = jnp.where(jnp.isfinite(amax), amax, 0.0)
        e = jnp.exp(alpha - amax[col])
        s = jax.ops.segment_sum(e, col, num_segments=num_nodes)
        alpha = e / (s[col] + 1e-16)
        msg = x_j * alpha[:, :, None]
        out = jax.ops.segment_sum(msg, col, num_segments=num_nodes)
        return out.reshape(num_nodes, HEADS * OUT_CH)
    edge_index = jnp.stack([src, dst])
    h = jnp.maximum(_layernorm(x, axis=-1), 0.0)
    x = x + _L0_gnn_ref(h, edge_index)
    h = jnp.maximum(_layernorm(x, axis=-1), 0.0)
    x = x + _L1_gnn_ref(h, edge_weight1, L1_gnn_W, L1_gnn_b, edge_index)
    h = jnp.maximum(_layernorm(x, axis=-1), 0.0)
    x = x + _L2_gnn_ref(h, edge_index, edge_type_9, 6250, L2_gnn_W_msg, L2_gnn_b_msg, L2_gnn_edge_embed, L2_gnn_W_ih, L2_gnn_W_hh, L2_gnn_b_ih, L2_gnn_b_hh)
    h = jnp.maximum(_layernorm(x, axis=-1), 0.0)
    x = x + _L3_gnn_ref(h, L3_gnn_weight, L3_gnn_att, edge_index)
    return x

_drawn_inputs = setup_inputs


def setup_inputs(seed=0):
    import zlib

    import numpy as np

    out = dict(_drawn_inputs(seed))
    spreads = {'L1_gnn_b': (0.0, 0.8)}
    factors = {'edge_weight1': 33.621,
     'L2_gnn_b_msg': 4.701,
     'L2_gnn_W_hh': 8.0,
     'L2_gnn_b_ih': 64.0,
     'L2_gnn_b_hh': 64.0,
     'L3_gnn_att': 64.0}
    for name, (base, spread) in spreads.items():
        noise = np.random.default_rng([zlib.crc32(name.encode()), seed]).standard_normal(out[name].shape)
        drawn = base * np.exp(spread * noise) if base else spread * noise
        out[name] = jnp.asarray(drawn.astype(out[name].dtype))
    for name, factor in factors.items():
        out[name] = (out[name] * factor).astype(out[name].dtype)
    return out
```

```python
from contextlib import ExitStack

import concourse.bass as bass
from concourse import mybir
from concourse.alu_op_type import AluOpType as ALU

ACT = mybir.ActivationFunctionType
F32 = mybir.dt.float32
BF16 = mybir.dt.bfloat16
I32 = mybir.dt.int32
AX = mybir.AxisListType.X
DVE_ENGINE = mybir.EngineType.DVE


def ceil_div(a, b):
    return -(-a // b)


def build(nc, x, src, dst, edge_type, edge_weight, mean_w, mean_b, msg_w, msg_b, embed, w_ih, w_hh,
          b_ih, b_hh, att_w, att, out):
    P = 128
    NODES, D = x.shape
    (EDGES,) = src.shape
    BLOCKS = ceil_div(NODES, P)
    LAST = NODES - (BLOCKS - 1) * P
    NPAD = BLOCKS * P
    CHUNKS = ceil_div(EDGES, P)
    EPAD = CHUNKS * P
    TAIL = EPAD - EDGES
    RING = 16
    HALF = RING // 2
    ITERS = ceil_div(CHUNKS + BLOCKS - 1, RING)
    STEPS = ITERS * RING
    CT = ceil_div(CHUNKS, P)
    CREST = CHUNKS - (CT - 1) * P
    KT = ceil_div(STEPS, P)
    KW = KT * P
    TYPES = embed.shape[0]
    ROW = D + TYPES
    NOBODY = 1 << 20
    EPS = 1e-5
    HEADS = att.shape[1]
    C = att.shape[2] // 2
    HA = 2 * HEADS
    ROW3 = D + HA
    BIG = 1.0e38
    IT3 = 33
    COLS3 = 2 * RING
    ONEHOT_COLS = IT3 * COLS3
    GATHER_COLS = CHUNKS - ONEHOT_COLS
    ROUNDS3 = ceil_div(GATHER_COLS, RING)
    TAIL3 = GATHER_COLS - (ROUNDS3 - 1) * RING
    G3 = 4
    GROUPS3 = COLS3 // G3
    HB = HEADS * BLOCKS
    LNG = 7
    NLN = BLOCKS // LNG
    COPIES = 8
    MROW = D + 1
    Q = 4
    GROUPS = STEPS // Q
    PIECE = 6
    PIECES = ceil_div(BLOCKS, PIECE)
    OUTSIDE = 200.0
    QW = 256
    NQ = ceil_div(NPAD, QW)
    NATT = ceil_div(BLOCKS, 3)
    WL = 16 * (11 + 2 * HEADS)
    assert D == P and BLOCKS % LNG == 0 and KT == CT and ROUNDS3 <= IT3 and TAIL3 > 0

    ctx = ExitStack()
    with ctx:
        def sb(name, shape, dt=F32):
            return ctx.enter_context(nc.sbuf_tensor(name, shape, dt))

        def sem(name):
            return ctx.enter_context(nc.semaphore(name))

        def dram(name, shape, dt=F32):
            return nc.dram_tensor(name, shape, dt).ap()

        dst_pad = dram("dst_pad", (EPAD,), I32)
        src_pad = dram("src_pad", (EPAD,), I32)
        type_pad = dram("type_pad", (EPAD,), I32)
        weight_pad = dram("weight_pad", (EPAD,), F32)
        tables = [dram(f"table{n}", (NPAD, D)) for n in range(2)]
        edge_rows = dram("edge_rows", (KW, 3, P), BF16)
        back = [dram(f"back{n}", (NPAD + P, MROW)) for n in range(COPIES)]
        low_rows = dram("low_rows", (KW, P), BF16)
        logit_table = dram("logit_table", (NPAD, HA))
        start_logits = dram("start_logits", (EPAD, HEADS))
        sums_dram = dram("sums_dram", (EPAD, HEADS))

        X = sb("X", [P, BLOCKS, D])
        acc = sb("acc", [P, BLOCKS * ROW])
        big = sb("big", [P, 2 * NPAD])
        hT = big[:, 0:NPAD]
        msg = big[:, NPAD:2 * NPAD]
        H = sb("H", [P, BLOCKS, D])
        dst_rel = sb("dst_rel", [P, KW])
        src_idx = sb("src_idx", [P, KW], I32)
        w_step = sb("w_step", [P, KW])
        type_step = sb("type_step", [P, KW])
        ring = sb("ring", [P, RING, ROW])
        onehot = sb("onehot", [P, RING, P])
        idx_stage = sb("idx_stage", [P, RING], I32)
        iota_k = sb("iota_k", [P, KW])
        pidx = sb("pidx", [P, 1])
        minus_p = sb("minus_p", [P, 1])
        kcol = sb("kcol", [P, KT])

        ident = sb("ident", [P, P])
        tri = sb("tri", [P, P])
        ones = sb("ones", [P, P])
        pad_i = sb("pad_i", [1, TAIL], I32)
        pad_z = sb("pad_z", [1, TAIL], I32)
        pad_f = sb("pad_f", [1, TAIL], F32)
        first_dst = sb("first_dst", [P, CT], I32)
        prev_dst = sb("prev_dst", [P, CT], I32)
        fb_i = sb("fb_i", [P, CT], I32)
        pb_i = sb("pb_i", [P, CT], I32)
        fb = sb("fb", [P, CT])
        pb = sb("pb", [P, CT])
        adv = sb("adv", [P, CT])
        adv_sum = sb("adv_sum", [P, CT])
        one13 = sb("one13", [P, BLOCKS])
        start_step = sb("start_step", [P, CT])
        pad_start = sb("pad_start", [P, 1])
        vw = sb("vw", [P, CT, 2], BF16)
        chunk_idx = sb("chunk_idx", [P, KT], I32)
        blk = sb("blk", [P, KT])
        neg_base = sb("neg_base", [P, KT])
        brow = sb("brow", [1, KW])
        off_row = sb("off_row", [1, KW], I32)
        stats = sb("stats", [P, BLOCKS, 6])
        mv = sb("mv", [P, BLOCKS, 2])
        ve = sb("ve", [P, BLOCKS])
        sd = sb("sd", [P, BLOCKS])
        rstd = sb("rstd", [P, BLOCKS])
        nmr = sb("nmr", [P, BLOCKS])
        types_at = sb("types_at", [P, BLOCKS, TYPES])
        typesT = H[0:TYPES, :, :].rearrange("p b f -> p (b f)")
        degree = sb("degree", [P, BLOCKS])
        rcount = sb("rcount", [P, BLOCKS])
        dump = sb("dump", [P, 1])
        rows3 = sb("rows3", [3, RING, P], BF16)
        pick = sb("pick", [3, 2, P], BF16)
        equals = sb("equals", [P, RING])
        src_less = sb("src_less", [P, RING])
        last_src = sb("last_src", [P, RING])
        total = sb("total", [P, BLOCKS])
        before = sb("before", [P, BLOCKS])
        upto = sb("upto", [P, BLOCKS])
        empty = sb("empty", [P, BLOCKS])
        begin_f = sb("begin_f", [P, BLOCKS])
        begin_i = sb("begin_i", [P, BLOCKS], I32)
        end_i = sb("end_i", [P, BLOCKS], I32)
        w_mean = sb("w_mean", [P, 2, D])
        b_mean = sb("b_mean", [P, D])
        w_raw = msg[:, 0:8 * D].rearrange("p (g f) -> p g f", g=8)
        wT = sb("wT", [P, 8, D])
        emb = sb("emb", [TYPES, D])
        emb_b = sb("emb_b", [TYPES, D])
        bcol = sb("bcol", [P, 6])
        brz = sb("brz", [P, 2])
        att_cols = sb("att_cols", [P, HA])
        w3 = sb("w3", [P, ROW3])
        gate = acc[:, 0:8 * QW].rearrange("p (a g w) -> p a g w", a=2, g=4)
        stage3 = onehot[:, :, :].rearrange("p a b -> p (a b)")[:, KW:KW + RING * HA].rearrange("p (u h) -> p u h", u=RING)
        first3 = first_dst[:, 0:1]
        first_logits = sb("first_logits", [P, HA])
        row_ends = type_step[:, 8 * P + 2 * BLOCKS * HEADS:8 * P + (2 * BLOCKS + 4) * HEADS]
        rowT = type_step[0:HEADS, 0:8 * P].rearrange("h (a p) -> h a p", a=8)
        carry = type_step[:, 8 * P + (2 * BLOCKS + 4) * HEADS:8 * P + (2 * BLOCKS + 6) * HEADS]
        sumsN = type_step[:, 8 * P:8 * P + BLOCKS * HEADS].rearrange("p (b h) -> p b h", h=HEADS)
        ratio = type_step[:, 8 * P + BLOCKS * HEADS:8 * P + 2 * BLOCKS * HEADS].rearrange("p (b h) -> p b h", h=HEADS)
        PS = ctx.enter_context(nc.psum_tensor("PS", [P, 8, 512], F32))

        consts_set = sem("consts_set")
        copied = sem("copied")
        x_loaded = sem("x_loaded")
        ends_loaded = sem("ends_loaded")
        w_loaded = sem("w_loaded")
        dve_done = sem("dve_done")
        att_folded = sem("att_folded")
        adv_ready = sem("adv_ready")
        adv_summed = sem("adv_summed")
        steps_marked = sem("steps_marked")
        steps_summed = sem("steps_summed")
        chunks_known = sem("chunks_known")
        rows_gathered = [sem(f"rows_gathered{n}") for n in range(4)]
        rows_ready = [sem(f"rows_ready{n}") for n in range(3)]
        rows_turned = sem("rows_turned")
        rows_stored = sem("rows_stored")
        zeros_ready = sem("zeros_ready")
        logits_zeroed = sem("logits_zeroed")
        ln_var = sem("ln_var")
        ln_sd = sem("ln_sd")
        ln_scale = sem("ln_scale")
        ln_relu = sem("ln_relu")
        table_written = sem("table_written")
        h_turned = sem("h_turned")
        h_stored = sem("h_stored")
        staged = sem("staged")
        pool_passed = sem("pool_passed")
        gathered = [sem(f"gathered{u}") for u in range(RING)]
        parts_made = sem("parts_made")
        rows_parted = sem("rows_parted")
        backs_zeroed = sem("backs_zeroed")
        rows3_loaded = [sem(f"rows3_loaded{q}") for q in range(RING // Q)]
        spread = sem("spread")
        same_raw = sem("same_raw")
        picks_ready = sem("picks_ready")
        same_ready = sem("same_ready")
        equals_ready = sem("equals_ready")
        less_ready = sem("less_ready")
        void_marked = sem("void_marked")
        places_ready = sem("places_ready")
        rows_picked = sem("rows_picked")
        rows_weighted = sem("rows_weighted")
        equals_summed = sem("equals_summed")
        sums_taken = sem("sums_taken")
        scattered = [sem(f"scattered{n}") for n in range(COPIES)]
        pieces_loaded = [sem(f"pieces_loaded{n}") for n in range(2)]
        piece_added = sem("piece_added")
        mean_ready = sem("mean_ready")
        mean_turned = sem("mean_turned")
        mean_stored = sem("mean_stored")
        hot_ready = sem("hot_ready")
        summed = sem("summed")
        added = sem("added")
        degree_ready = sem("degree_ready")
        nodes_summed = sem("nodes_summed")
        nodes_counted = sem("nodes_counted")
        types_turned = sem("types_turned")
        types_stored = sem("types_stored")
        w_turned = sem("w_turned")
        wT_ready = sem("wT_ready")
        mean_summed = sem("mean_summed")
        mean_added = sem("mean_added")
        msg_summed = sem("msg_summed")
        msg_stored = sem("msg_stored")
        gates_summed = sem("gates_summed")
        rz_ready = sem("rz_ready")
        n_summed = sem("n_summed")
        n_ready = sem("n_ready")
        gru_ready = sem("gru_ready")
        gru_turned = sem("gru_turned")
        gru_added = sem("gru_added")
        att_summed = sem("att_summed")
        att_stored = sem("att_stored")
        w3_ready = sem("w3_ready")
        logits_written = sem("logits_written")
        starts_written = sem("starts_written")
        last_loaded = sem("last_loaded")
        first_back = sem("first_back")
        filled_back = sem("filled_back")
        staged3 = sem("staged3")
        gathered3 = [sem(f"gathered3_{q}") for q in range(RING // G3)]
        ring_cleared = sem("ring_cleared")
        src3_loaded = sem("src3_loaded")
        low_made = sem("low_made")
        low_turned = sem("low_turned")
        low_ready = sem("low_ready")
        low_stored = sem("low_stored")
        lows_loaded = [sem(f"lows_loaded{n}") for n in range(2)]
        parts3_ready = sem("parts3_ready")
        low_spread = sem("low_spread")
        low_apart = sem("low_apart")
        low_hot = sem("low_hot")
        high_hot = sem("high_hot")
        picked3 = sem("picked3")
        multiplied3 = sem("multiplied3")
        picked_logits = sem("picked_logits")
        all_logits = sem("all_logits")
        ends_turn = sem("ends_turn")
        turned3 = sem("turned3")
        carry_row = sem("carry_row")
        exp_in = sem("exp_in")
        exp_out = sem("exp_out")
        sums_ready = sem("sums_ready")
        sums_written = sem("sums_written")
        sums_back = sem("sums_back")
        out_ready = sem("out_ready")
        out_written = sem("out_written")

        HWv = acc[:, 0:BLOCKS * ROW3].rearrange("p (b r) -> p b r", r=ROW3)
        al = hT[:, 0:CHUNKS * HEADS]
        al3 = al.rearrange("p (j h) -> p j h", h=HEADS)
        aj = H[:, :, :].rearrange("p b f -> p (b f)")[:, 0:CHUNKS * HEADS]
        aj3 = aj.rearrange("p (j h) -> p j h", h=HEADS)
        mx = msg[:, 0:CHUNKS * HEADS]
        mx3 = mx.rearrange("p (j h) -> p j h", h=HEADS)
        flat_ring = ring[:, :, :].rearrange("p a b -> p (a b)")
        flat_hot = onehot[:, :, :].rearrange("p a b -> p (a b)")
        dst3 = flat_ring[:, 0:CHUNKS].bitcast(I32)
        prev3 = flat_hot[:, 0:CHUNKS].bitcast(I32)
        not_start = w_step[:, 0:CHUNKS]
        start_low = dst_rel[:, 0:CHUNKS]
        src3 = src_idx[:, 0:CHUNKS]
        AN = CHUNKS * HEADS
        raw3 = flat_ring[:, 0:KW].bitcast(I32)
        low_i = flat_hot[:, 0:KW].bitcast(I32)
        lowT = flat_hot[:, 0:KW // 2].bitcast(BF16)
        products = msg[:, 0:4 * G3 * HB].rearrange("p (n s m) -> p n s m", n=2, m=HB)
        highs = msg[:, 4 * G3 * HB:4 * G3 * (HB + BLOCKS)].rearrange("p (n s b) -> p n s b", n=2, b=BLOCKS)
        at3 = 4 * G3 * (HB + BLOCKS)
        apart = msg[:, at3:at3 + G3 * P].bitcast(BF16).rearrange("p (n k) -> p n k", n=2)
        low_hots = msg[:, at3 + G3 * P:at3 + 2 * G3 * P].bitcast(BF16).rearrange("p (n k) -> p n k", n=2)
        lows = msg[0:1, at3 + 2 * G3 * P:at3 + 4 * G3 * P].bitcast(BF16).rearrange("p (n s e) -> p n s e", n=2, e=P)
        parts3 = msg[:, at3 + 4 * G3 * P:at3 + 4 * G3 * P + 3 * HB // 2].bitcast(BF16).rearrange("p (a m) -> p a m", a=3)
        left3 = products[:, 0, 0, :]
        ones_row = flat_ring[0:1, KW:KW + P // 2].bitcast(BF16)

        dstT = onehot[:, 0:2 * Q, :]
        same = onehot[:, 2 * Q:4 * Q, :]
        picked = flat_ring[:, 0:2 * Q * MROW].rearrange("p (s r) -> p s r", r=MROW)
        sums_out = flat_ring[:, 2 * Q * MROW:(2 * Q + COPIES) * MROW].rearrange("p (s r) -> p s r", r=MROW)
        in_block = type_step
        acc_m = acc[:, 0:BLOCKS * MROW].rearrange("p (b r) -> p b r", r=MROW)
        pieces = [H[:, :, :].rearrange("p b f -> p (b f)"), msg]
        rows3_bf = hT[:, 0:3 * KW // 2].bitcast(BF16).rearrange("p (a k) -> p a k", a=3)
        src_high = hT[:, 3 * KW // 2:5 * KW // 2].bitcast(I32)
        src_low = hT[:, 5 * KW // 2:7 * KW // 2].bitcast(I32)

        marks = big[:, :].bitcast(BF16)[:, 0:CT * KW].rearrange("p (t k) -> p t k", k=KW)
        rows = [acc[:, n * KW:(n + 1) * KW] for n in range(4)]
        rows_i = [r.bitcast(I32) for r in rows]
        acc_d = acc[:, 0:NPAD]
        h_flat = H[:, :, :].rearrange("p b f -> p (b f)")

        def slot(u, w):
            return PS[:, u // 2, (u % 2) * 256:(u % 2) * 256 + w]

        block = ctx.enter_context(nc.Block())

        @block.sync
        def _(sp):
            sp.wait_ge(consts_set, 1)
            for full, pad, tail in ((dst_pad, dst, pad_i), (src_pad, src, pad_z), (type_pad, edge_type, pad_z),
                                    (weight_pad, edge_weight, pad_f)):
                sp.dma_start(full[0:EDGES].rearrange("(a b) -> a b", a=16), pad.rearrange("(a b) -> a b", a=16)
                             ).then_inc(copied, 16)
                sp.dma_start(full[EDGES:EPAD].rearrange("(a b) -> a b", a=1), tail[:, :]).then_inc(copied, 16)
            whole = (BLOCKS - 1) * P
            sp.wait_ge(ring_cleared, 1)
            sp.dma_start(raw3[0:P - 1, 0:CHUNKS], src[0:(P - 1) * CHUNKS].rearrange("(p j) -> p j", p=P - 1)
                         ).then_inc(src3_loaded, 16)
            sp.dma_start(raw3[P - 1:P, 0:CHUNKS - TAIL], src[(P - 1) * CHUNKS:EDGES].rearrange("(p j) -> p j", p=1)
                         ).then_inc(src3_loaded, 16)
            sp.dma_start(X[:, 0:BLOCKS - 1, :], x[0:whole, :].rearrange("(b p) f -> p b f", p=P)).then_inc(x_loaded, 16)
            sp.dma_start(X[0:LAST, BLOCKS - 1, :], x[whole:NODES, :]).then_inc(x_loaded, 16)
            sp.dma_start(w_mean[:, :, :], mean_w.rearrange("(a f) o -> f a o", a=2)).then_inc(w_loaded, 16)
            sp.dma_start(b_mean[:, :], mean_b.rearrange("(a o) -> a o", a=1).broadcast_to([P, D])
                         ).then_inc(w_loaded, 16)
            sp.dma_start(w3[:, 0:D], att_w).then_inc(w_loaded, 16)
            sp.dma_start(emb[:, :], embed).then_inc(w_loaded, 16)
            sp.dma_start(emb_b[:, :], msg_b.rearrange("(a o) -> a o", a=1).broadcast_to([TYPES, D])).then_inc(w_loaded, 16)
            with nc.allow_non_contiguous_dma("a few columns of biases"):
                sp.dma_start(bcol[:, 0:3], b_ih.rearrange("(g j) -> j g", g=3)).then_inc(w_loaded, 16)
                sp.dma_start(bcol[:, 3:6], b_hh.rearrange("(g j) -> j g", g=3)).then_inc(w_loaded, 16)
                for h in range(HEADS):
                    sp.dma_start(att_cols[h * C:(h + 1) * C, h:h + 1], att[0, h:h + 1, 0:C].rearrange("a c -> c a")
                                 ).then_inc(w_loaded, 16)
                    sp.dma_start(att_cols[h * C:(h + 1) * C, HEADS + h:HEADS + h + 1],
                                 att[0, h:h + 1, C:2 * C].rearrange("a c -> c a")).then_inc(w_loaded, 16)
            def write_table(n, norm):
                for g in range(NLN):
                    sp.wait_ge(ln_relu, NLN * norm + g + 1)
                    b0 = g * LNG
                    sp.dma_start(tables[n][b0 * P:(b0 + LNG) * P, :].rearrange("(b p) f -> p b f", p=P),
                                 H[:, b0:b0 + LNG, :]).then_inc(table_written, 16)

            sp.wait_ge(low_ready, 1)
            sp.dma_start(low_rows.rearrange("(t p) e -> p t e", p=P), lowT.rearrange("p (t e) -> p t e", e=P)
                         ).then_inc(low_stored, 16)
            write_table(0, 0)
            sp.wait_ge(parts_made, 1)
            for a in range(3):
                sp.dma_start(edge_rows[:, a, :].rearrange("(t p) e -> p t e", p=P),
                             rows3_bf[:, a, :].rearrange("p (t e) -> p t e", e=P)).then_inc(rows_parted, 16)
            sp.wait_ge(zeros_ready, 1)
            for n in range(COPIES):
                half = (NPAD + P) // 2 * MROW
                for v in range(2):
                    sp.dma_start(back[n].rearrange("k r -> (k r)")[v * half:(v + 1) * half].rearrange("(p m) -> p m", p=P),
                                 msg[:, 0:half // P]).then_inc(backs_zeroed, 16)
            sp.dma_start(start_logits.rearrange("(p j) h -> p (j h)", p=P), mx).then_inc(logits_zeroed, 16)
            sp.wait_ge(logits_zeroed, 16)
            sp.wait_ge(backs_zeroed, 32 * COPIES)
            sp.dma_start(w_raw[:, 0, :], msg_w).then_inc(w_loaded, 16)
            sp.dma_start(w_raw[:, 1:4, :], w_ih.rearrange("(g j) f -> j g f", g=3)).then_inc(w_loaded, 16)
            sp.dma_start(w_raw[:, 4:7, :], w_hh.rearrange("(g j) f -> j g f", g=3)).then_inc(w_loaded, 16)
            sp.dma_start(w_raw[:, 7, :], att_w).then_inc(w_loaded, 16)
            sp.wait_ge(rows_parted, 48)

            def load_rows3(i, q):
                sp.dma_start(rows3[:, q * Q:(q + 1) * Q, :],
                             edge_rows[bass.ds(i * RING + q * Q, Q), :, :].rearrange("k a e -> a k e")
                             ).then_inc(rows3_loaded[q], 16)

            for q in range(RING // Q):
                load_rows3(0, q)
            with sp.Fori(0, ITERS - 1) as i:
                for q in range(RING // Q):
                    sp.wait_ge(spread, i * (RING // Q) + (q + 1))
                    load_rows3(i + 1, q)
            for n in range(COPIES):
                sp.wait_ge(scattered[n], 32 * ITERS)
            for c in range(PIECES):
                b0, nb = c * PIECE, min(PIECE, BLOCKS - c * PIECE)
                if c >= 2:
                    sp.wait_ge(piece_added, c - 1)
                to = pieces[c % 2][:, 0:COPIES * nb * MROW].rearrange("p (n b r) -> p n b r", n=COPIES, r=MROW)
                for n in range(COPIES):
                    sp.dma_start(to[:, n, :, :], back[n][b0 * P:(b0 + nb) * P, :].rearrange("(b p) r -> p b r", p=P)
                                 ).then_inc(pieces_loaded[c % 2], 16)
            write_table(1, 2)
            sp.wait_ge(added, 2 * STEPS)
            sp.wait_ge(summed, 2 * STEPS)
            sp.wait_ge(staged, 2 * ITERS * 2)
            sp.dma_start(dst3, dst_pad.rearrange("(p j) -> p j", p=P)).then_inc(last_loaded, 16)
            sp.dma_start(prev3[1:P, :], dst_pad[CHUNKS - 1:EPAD - 1].rearrange("(p j) -> p j", p=P - 1)
                         ).then_inc(last_loaded, 16)
            sp.dma_start(prev3[0:1, 1:CHUNKS], dst_pad[0:CHUNKS - 1].rearrange("(p j) -> p j", p=1)
                         ).then_inc(last_loaded, 16)
            with nc.allow_non_contiguous_dma("the first destination of each row"):
                sp.dma_start(first3[:, :], dst_pad.rearrange("(p j) -> p j", p=P)[:, 0:1]).then_inc(last_loaded, 16)
            sp.dma_start(src3[:, 0:CHUNKS], src_pad.rearrange("(p j) -> p j", p=P)).then_inc(last_loaded, 16)
            sp.wait_ge(att_stored, NATT)
            sp.dma_start(logit_table.rearrange("(b p) h -> p b h", p=P), HWv[:, :, D:ROW3]).then_inc(logits_written, 16)

            def load_lows(i, m):
                sp.dma_start(lows[:, m % 2, :, :], low_rows[bass.ds(i * COLS3 + m * 2 * G3, 2 * G3), :].unsqueeze(0)
                             ).then_inc(lows_loaded[m % 2], 16)

            def low_round(i, first):
                for m in range(first, COLS3 // (2 * G3)):
                    sp.wait_ge(low_spread, i * GROUPS3 + 2 * (m - 1))
                    load_lows(i, m)

            for m in range(2):
                load_lows(0, m)
            low_round(0, 2)
            with sp.Fori(1, IT3) as i:
                low_round(i, 0)
            sp.wait_ge(starts_written, 16 * BLOCKS)
            sp.dma_start(aj, start_logits.rearrange("(p j) h -> p (j h)", p=P)).then_inc(filled_back, 16)
            sp.wait_ge(sums_ready, 1)
            sp.dma_start(sums_dram.rearrange("(p j) h -> p (j h)", p=P), mx).then_inc(sums_written, 16)
            sp.wait_ge(out_ready, 1)
            sp.dma_start(out[0:whole, :].rearrange("(b p) f -> p b f", p=P), X[:, 0:BLOCKS - 1, :]).then_inc(out_written, 16)
            sp.dma_start(out[whole:NODES, :], X[0:LAST, BLOCKS - 1, :]).then_inc(out_written, 16)
            sp.wait_ge(out_written, 32)

        @block.gpsimd
        def _(pool):
            pool.memset(pad_i[:, :], NOBODY)
            pool.memset(pad_z[:, :], 0)
            pool.memset(att_cols[:, :], 0.0)
            pool.memset(X[:, BLOCKS - 1, :], 0.0)
            pool.memset(pad_f[:, :], 0.0).then_inc(consts_set, 1)
            pool.iota(iota_k[:, :], pattern=[[1, KW]], base=0, channel_multiplier=0,
                      allow_small_or_imprecise_dtypes=True)
            pool.iota(pidx[:, :], pattern=[[0, 1]], base=0, channel_multiplier=1, allow_small_or_imprecise_dtypes=True)
            pool.iota(kcol[:, :], pattern=[[P, KT]], base=0, channel_multiplier=1,
                      allow_small_or_imprecise_dtypes=True).then_inc(consts_set, 1)
            pool.memset(first_dst[:, :], 0)
            pool.memset(prev_dst[:, :], -P).then_inc(consts_set, 1)
            pool.wait_ge(consts_set, 3)
            pool.wait_ge(copied, 128)
            body = (CT - 1) * P * P
            with nc.allow_non_contiguous_dma("one number of each chunk"):
                pool.dma_start(first_dst[:, 0:CT - 1], dst_pad[0:body].rearrange("(t p e) -> p t e", p=P, e=P)[:, :, 0]
                               ).then_inc(ends_loaded, 16)
                pool.dma_start(first_dst[0:CREST, CT - 1:CT], dst_pad[body:EPAD].rearrange("(p e) -> p e", e=P)[:, 0:1]
                               ).then_inc(ends_loaded, 16)
                y = dst_pad[P - 1:EPAD - 1]
                pool.dma_start(prev_dst[1:P, 0:1], y[0:(P - 1) * P].rearrange("(p e) -> p e", e=P)[:, 0:1]
                               ).then_inc(ends_loaded, 16)
                pool.dma_start(prev_dst[:, 1:CT - 1], y[(P - 1) * P:(P - 1) * P + (CT - 2) * P * P].rearrange(
                    "(t p e) -> p t e", p=P, e=P)[:, :, 0]).then_inc(ends_loaded, 16)
                z = (P - 1) * P + (CT - 2) * P * P
                pool.dma_start(prev_dst[0:CREST, CT - 1:CT], y[z:z + CREST * P].rearrange("(p e) -> p e", e=P)[:, 0:1]
                               ).then_inc(ends_loaded, 16)
            pool.wait_ge(chunks_known, 1)
            for n, pad in enumerate((dst_pad, src_pad, type_pad, weight_pad)):
                view = pad.rearrange("(c e) -> c e", e=P)
                dest = rows[n] if n == 3 else rows_i[n]
                for t in range(KT):
                    pool.indirect_dma_start(dest[:, t * P:(t + 1) * P], None, view,
                                            bass.IndirectOffsetOnAxis(ap=chunk_idx[:, t:t + 1], axis=0)
                                            ).then_inc(rows_gathered[n], 16)

            def edge_gathers(turn):
                pool.wait_ge(table_written, 16 * NLN * (turn + 1))
                with pool.Fori(0, ITERS) as i:
                    for h in range(2):
                        pool.wait_ge(staged, i * 2 + (2 * ITERS * turn + h + 1))
                        pool.sem_inc(pool_passed, 1)
                        for u in range(h * HALF, (h + 1) * HALF):
                            pool.indirect_dma_start(ring[:, u, 0:D], None, tables[turn],
                                                    bass.IndirectOffsetOnAxis(ap=idx_stage[:, u:u + 1], axis=0)
                                                    ).then_inc(gathered[u], 16)

            edge_gathers(0)

            pool.wait_ge(backs_zeroed, 32 * COPIES)

            def scatter(q):
                for s in range(Q):
                    u = q * Q + s
                    pool.indirect_dma_start(back[u % COPIES], bass.IndirectOffsetOnAxis(ap=idx_stage[:, u:u + 1], axis=0),
                                            sums_out[:, u % COPIES, :], None, compute_op=ALU.add
                                            ).then_inc(scattered[u % COPIES], 16)

            with pool.Fori(0, ITERS) as i:
                for q in range(RING // Q):
                    pool.wait_ge(sums_taken, i * (RING // Q) + (q + 1))
                    pool.sem_inc(pool_passed, 1)
                    scatter(q)

            edge_gathers(1)

            pool.wait_ge(logits_zeroed, 16)
            pool.wait_ge(att_stored, NATT)
            pool.wait_ge(nodes_counted, 1)
            for b in range(BLOCKS):
                pool.indirect_dma_start(start_logits, bass.IndirectOffsetOnAxis(ap=begin_i[:, b:b + 1], axis=0),
                                        HWv[:, b, D + HEADS:ROW3], None, bounds_check=EPAD - 1, oob_is_err=False
                                        ).then_inc(starts_written, 16)
            pool.wait_ge(logits_written, 16)
            pool.wait_ge(last_loaded, 80)
            pool.indirect_dma_start(first_logits[:, :], None, logit_table,
                                    bass.IndirectOffsetOnAxis(ap=first3[:, 0:1], axis=0)).then_inc(first_back, 16)

            def gather_round(i, columns):
                for q in range(ceil_div(columns, G3)):
                    pool.wait_ge(staged3, i * (RING // G3) + (q + 1))
                    pool.sem_inc(pool_passed, 1)
                    for u in range(q * G3, min(columns, (q + 1) * G3)):
                        pool.indirect_dma_start(stage3[:, u, :], None, logit_table,
                                                bass.IndirectOffsetOnAxis(ap=idx_stage[:, u:u + 1], axis=0)
                                                ).then_inc(gathered3[q], 16)

            with pool.Fori(0, ROUNDS3 - 1) as i:
                gather_round(i, RING)
            gather_round(ROUNDS3 - 1, TAIL3)
            pool.wait_ge(sums_written, 16)
            for b in range(BLOCKS):
                pool.indirect_dma_start(sumsN[:, b, :], None, sums_dram,
                                        bass.IndirectOffsetOnAxis(ap=end_i[:, b:b + 1], axis=0),
                                        bounds_check=EPAD - 1, oob_is_err=False).then_inc(sums_back, 16)

        @block.scalar
        def _(act):
            def layer_norm(n, turn):
                for g in range(NLN):
                    b0 = g * LNG
                    act.wait_ge(ln_var, NLN * n + g + 1)
                    act.activation(sd[:, b0:b0 + LNG], ve[:, b0:b0 + LNG], ACT.Sqrt).then_inc(ln_sd, 1)
                    act.wait_ge(ln_scale, NLN * n + g + 1)
                    if g == 0 and n:
                        act.wait_ge(table_written, 16 * NLN * (1 if n < 3 else 2))
                    for b in range(b0, b0 + LNG):
                        ins = act.activation(H[:, b, :], X[:, b, :], ACT.Relu, bias=nmr[:, b:b + 1], scale=rstd[:, b:b + 1])
                    ins.then_inc(ln_relu, 1)
                if turn:
                    for q in range(ceil_div(BLOCKS, 4)):
                        w = min(4, BLOCKS - 4 * q) * P
                        act.wait_ge(h_turned, ceil_div(BLOCKS, 4) * (n - 1) + q + 1)
                        act.activation(hT[:, q * 512:q * 512 + w], PS[:, q % 8, 0:w], ACT.Copy).then_inc(h_stored, 1)

            def edge_stages(turn):
                def stage(i, h):
                    act.activation(idx_stage[:, h * HALF:(h + 1) * HALF], src_idx[:, bass.ds(i * RING + h * HALF, HALF)],
                                   ACT.Copy).then_inc(staged, 1)

                for h in range(2):
                    stage(0, h)
                with act.Fori(0, ITERS - 1) as i:
                    for h in range(2):
                        act.wait_ge(summed, i * RING + (STEPS * turn + (h + 1) * HALF))
                        stage(i + 1, h)

            act.wait_ge(low_turned, 1)
            act.activation(lowT, PS[:, 4:8, :].rearrange("p a b -> p (a b)")[:, 0:KW], ACT.Copy).then_inc(low_ready, 1)
            layer_norm(0, False)
            act.wait_ge(parts_made, 1)
            act.activation(rows[1], rows_i[1], ACT.Copy).then_inc(rows_ready[1], 1)

            def turned_out(n, dest, want):
                act.wait_ge(rows_turned, want)
                base = 4 * (n % 2)
                flat = PS[:, base:base + 4, :].rearrange("p a b -> p (a b)")
                act.activation(dest[:, 0:KW], flat[:, 0:KW], ACT.Copy).then_inc(rows_stored, 1)

            turned_out(0, dst_rel, 1)
            turned_out(1, src_idx, 2)
            turned_out(2, type_step, 3)
            turned_out(3, w_step, 4)

            edge_stages(0)
            for q in range(2):
                act.wait_ge(w_turned, q + 1)
                act.activation(wT[:, 4 * q:4 * q + 4, :].rearrange("p a b -> p (a b)"), PS[:, 2 + q, :], ACT.Copy
                               ).then_inc(wT_ready, 1)
            layer_norm(1, True)

            GI = RING // Q

            def weigh(i, q):
                act.wait_ge(rows_picked, i * GI + (q + 1))
                for s in range(Q):
                    act.activation(picked[:, (q % 2) * Q + s, 0:D], PS[:, 2 + q % 2, s * P:(s + 1) * P], ACT.Copy,
                                   scale=w_step[:, bass.ds(i * RING + (q * Q + s), 1)])
                act.activation(picked[:, (q % 2) * Q:(q % 2 + 1) * Q, D], in_block[:, bass.ds(i * RING + q * Q, Q)], ACT.Copy
                               ).then_inc(rows_weighted, 1)

            def take(i, q):
                act.wait_ge(equals_summed, i * GI + (q + 1))
                act.wait_ge(places_ready, i * GI + (q + 1))
                for s in range(0, Q, 2):
                    u = q * Q + s
                    for v in (u, u + 1):
                        if not (isinstance(i, int) and i == 0 and v < COPIES):
                            act.wait_ge(scattered[v % COPIES], i * 32 + 16 * (v // COPIES))
                    bank = 4 + 2 * (q % 2) + s // 2
                    ins = act.activation(sums_out[:, u % COPIES:u % COPIES + 2, :],
                                         PS[:, bank, :].rearrange("p (s r) -> p s r", s=2)[:, :, 0:MROW], ACT.Copy)
                ins.then_inc(sums_taken, 1)

            def back_round(i, first):
                for q in range(GI):
                    weigh(i, q)
                    if q or not first:
                        take(i if q else i - 1, (q - 1) % GI)

            back_round(0, True)
            with act.Fori(1, ITERS) as i:
                back_round(i, False)
            take(ITERS - 1, GI - 1)
            for q in range(ceil_div(BLOCKS, 4)):
                w = min(4, BLOCKS - 4 * q) * P
                act.wait_ge(mean_turned, q + 1)
                act.activation(msg[:, q * 512:q * 512 + w], PS[:, q % 4, 0:w], ACT.Copy).then_inc(mean_stored, 1)
            layer_norm(2, True)
            edge_stages(1)
            act.wait_ge(table_written, 16 * NLN * 2)
            for q in range(ceil_div(BLOCKS, 4)):
                w = min(4, BLOCKS - 4 * q) * P
                act.wait_ge(types_turned, q + 1)
                act.activation(typesT[:, q * 512:q * 512 + w], PS[0:TYPES, q % 8, 0:w], ACT.Copy).then_inc(types_stored, 1)
            for q in range(ceil_div(NPAD, 512)):
                w = min(512, NPAD - 512 * q)
                act.wait_ge(msg_summed, q + 1)
                act.activation(msg[:, q * 512:q * 512 + w], PS[:, q % 2, 0:w], ACT.Copy).then_inc(msg_stored, 1)
            for q in range(NQ):
                w = min(QW, NPAD - QW * q)
                act.wait_ge(gates_summed, q + 1)
                if q >= 2:
                    act.wait_ge(gru_turned, q - 1)
                pr = 2 + 2 * (q % 2)
                act.activation(gate[:, q % 2, 0, 0:w], PS[:, pr, 0:w], ACT.Sigmoid, bias=brz[:, 0:1]).then_inc(rz_ready, 1)
                act.activation(gate[:, q % 2, 1, 0:w], PS[:, pr, QW:QW + w], ACT.Sigmoid, bias=brz[:, 1:2]).then_inc(rz_ready, 1)
                act.wait_ge(n_summed, q + 1)
                act.activation(gate[:, q % 2, 2, 0:w], gate[:, q % 2, 3, 0:w], ACT.Tanh, bias=bcol[:, 2:3]).then_inc(n_ready, 1)
            layer_norm(3, True)
            for q in range(ceil_div(BLOCKS, 3)):
                k = min(3, BLOCKS - 3 * q)
                act.wait_ge(att_summed, q + 1)
                ins = act.activation(HWv[:, 3 * q:3 * q + k, :].rearrange("p b r -> p (b r)"), PS[:, q % 8, 0:k * ROW3], ACT.Copy)
                ins.then_inc(att_stored, 1)

            act.wait_ge(last_loaded, 80)

            def quarter(i, q):
                if isinstance(i, int) and i >= ROUNDS3 - 1:
                    return min(G3, max(0, TAIL3 - q * G3)) if i == ROUNDS3 - 1 else 0
                return G3

            def stage3_in(i, q):
                k = quarter(i, q)
                if k:
                    act.activation(idx_stage[:, q * G3:q * G3 + k], src3[:, bass.ds(i * RING + (ONEHOT_COLS + q * G3), k)],
                                   ACT.Copy).then_inc(staged3, 1)

            def stage3_out(i, q):
                k = quarter(i, q)
                if k:
                    act.wait_ge(gathered3[q], i * (16 * G3) + 16 * k)
                    act.activation(al3[:, bass.ds(i * RING + (ONEHOT_COLS + q * G3), k), :],
                                   stage3[:, q * G3:q * G3 + k, 0:HEADS], ACT.Copy).then_inc(all_logits, 1)

            def low_hots3(i, g):
                n = i * GROUPS3 + g
                act.wait_ge(low_spread, n + 1)
                act.activation(apart[:, g % 2, :], PS[:, g % 2, :], ACT.Abs, bias=minus_p[:, 0:1]).then_inc(low_apart, 1)
                act.wait_ge(low_apart, n + 1)
                if not (isinstance(i, int) and i == 0 and g < 2):
                    act.wait_ge(picked3, n - 1)
                act.activation(low_hots[:, g % 2, :], apart[:, g % 2, :], ACT.Relu, bias=1.0, scale=-1.0).then_inc(low_hot, 1)

            def logit_round(i):
                for q in range(RING // G3):
                    low_hots3(i, 2 * q)
                    low_hots3(i, 2 * q + 1)
                    stage3_out(i, q)
                    if not isinstance(i, int) or quarter(i + 1, q):
                        act.wait_ge(all_logits, i * (RING // G3) + (q + 1))
                        stage3_in(i + 1, q)

            for q in range(RING // G3):
                stage3_in(0, q)
            logit_round(0)
            with act.Fori(1, ROUNDS3 - 2) as i:
                logit_round(i)
            for i in range(ROUNDS3 - 2, IT3):
                logit_round(i)
            act.wait_ge(exp_in, 1)
            act.activation(aj, aj, ACT.Exp).then_inc(exp_out, 1)
            act.wait_ge(exp_in, 2)
            act.activation(al[:, 0:AN], al[:, 0:AN], ACT.Exp).then_inc(exp_out, 1)
            act.wait_ge(exp_in, 3)
            act.activation(rowT[:, 5, :], rowT[:, 5, :], ACT.Exp).then_inc(exp_out, 1)

        @block.tensor
        def _(pe):
            pe.wait_ge(low_made, 1)
            for t in range(KT):
                ins = pe.transpose(PS[:, 4 + t // 4, (t % 4) * P:(t % 4 + 1) * P], flat_ring[:, t * P:(t + 1) * P], ident[:, :])
            ins.then_inc(low_turned, 1)
            pe.wait_ge(adv_ready, 1)
            pe.matmul(PS[:, 0, 0:CT], tri[:, :], adv[:, :], start=True, stop=False)
            pe.matmul(PS[:, 0, 0:CT], ones[:, :], adv_sum[:, :], start=False, stop=True).then_inc(adv_summed, 1)
            pe.wait_ge(steps_marked, 1)
            pe.wait_ge(low_ready, 1)
            for k in range(KT):
                for t in range(CT):
                    pe.matmul(PS[:, 1, 2 * k:2 * k + 2], marks[:, t, k * P:(k + 1) * P], vw[:, t, :],
                              start=(t == 0), stop=(t == CT - 1))
            for s in range(4):
                for t in range(CT):
                    ins = pe.matmul(PS[0:1, 2 + s, 0:KW // 4], vw[:, t, 1:2], marks[:, t, s * (KW // 4):(s + 1) * (KW // 4)],
                                    start=(t == 0), stop=(t == CT - 1))
            ins.then_inc(steps_summed, 1)
            pe.wait_ge(chunks_known, 2)
            for n in range(4):
                if n < 3:
                    pe.wait_ge(rows_ready[n], 1)
                else:
                    pe.wait_ge(rows_gathered[3], 16 * KT)
                if n >= 2:
                    pe.wait_ge(rows_stored, n - 1)
                for t in range(KT):
                    ins = pe.transpose(PS[:, 4 * (n % 2) + t // 4, (t % 4) * P:(t % 4 + 1) * P], rows[n][:, t * P:(t + 1) * P],
                                       ident[:, :])
                ins.then_inc(rows_turned, 1)
            pe.wait_ge(rows_stored, 4)

            def turn_h(n):
                for q in range(ceil_div(BLOCKS, 4)):
                    if q >= 8:
                        pe.wait_ge(h_stored, ceil_div(BLOCKS, 4) * (n - 1) + q - 7)
                    k = min(4, BLOCKS - 4 * q)
                    pe.wait_ge(ln_relu, NLN * n + (4 * q + k - 1) // LNG + 1)
                    for j in range(k):
                        ins = pe.transpose(PS[:, q % 8, j * P:(j + 1) * P], H[:, 4 * q + j, :], ident[:, :])
                    ins.then_inc(h_turned, 1)
                pe.wait_ge(h_stored, ceil_div(BLOCKS, 4) * n)

            def edge_sums(turn):
                with pe.Fori(0, ITERS) as i:
                    for h in range(2):
                        pe.wait_ge(hot_ready, i * 2 + (2 * ITERS * turn + h + 1))
                        for u in range(h * HALF, (h + 1) * HALF):
                            pe.wait_ge(gathered[u], i * 16 + (16 * ITERS * turn + 16))
                            if turn == 0:
                                pe.matmul(slot(u, ROW), onehot[:, u, :], ring[:, u, :], start=True, stop=True
                                          ).then_inc(summed, 1)
                            else:
                                pe.matmul(slot(u, D), ring[:, u, 0:D], onehot[:, u, :], start=True, stop=True
                                          ).then_inc(summed, 1)
                pe.wait_ge(added, STEPS * (turn + 1))

            edge_sums(0)
            pe.wait_ge(degree_ready, 1)
            pe.matmul(PS[:, 0, 0:BLOCKS], tri[:, :], degree[:, :], start=True, stop=True)
            pe.matmul(PS[:, 1, 0:BLOCKS], ones[:, :], degree[:, :], start=True, stop=True).then_inc(nodes_summed, 1)
            pe.wait_ge(w_loaded, WL)
            for q in range(2):
                for j in range(4):
                    ins = pe.transpose(PS[:, 2 + q, j * P:(j + 1) * P], w_raw[:, 4 * q + j, :], ident[:, :])
                ins.then_inc(w_turned, 1)
            pe.wait_ge(wT_ready, 2)
            pe.matmul(PS[:, 4, 0:HA], wT[:, 7, :], att_cols[:, :], start=True, stop=True).then_inc(att_folded, 1)
            pe.wait_ge(w3_ready, 1)
            turn_h(1)

            GI = RING // Q

            def spread_group(i, q):
                pe.wait_ge(rows3_loaded[q], i * 16 + 16)
                if not (isinstance(i, int) and i == 0 and q == 0):
                    pe.wait_ge(same_raw, i * GI + q)
                r3 = rows3[:, q * Q:(q + 1) * Q, :].rearrange("a s e -> a (s e)")
                pe.matmul(PS[:, 0, :], pick[:, 0, :], r3, start=True, stop=True)
                pe.matmul(PS[:, 1, :], pick[:, 1, :], r3, start=True, stop=True).then_inc(spread, 1)

            def pick_rows(i, q, at):
                pe.wait_ge(picks_ready, i * GI + (q + 1))
                for s in range(Q):
                    ins = pe.matmul(PS[:, 2 + q % 2, s * P:(s + 1) * P], dstT[:, (q % 2) * Q + s, :],
                                    h_flat[:, bass.ds(at[q * Q + s], D)], start=True, stop=True)
                ins.then_inc(rows_picked, 1)

            def sum_equals(i, q):
                pe.wait_ge(rows_weighted, i * GI + (q + 1))
                pe.wait_ge(same_ready, i * GI + (q + 1))
                if not (isinstance(i, int) and i == 0 and q < 2):
                    pe.wait_ge(sums_taken, i * GI + (q - 1))
                for s in range(Q):
                    ins = pe.matmul(PS[:, 4 + 2 * (q % 2) + s // 2, (s % 2) * 256:(s % 2) * 256 + MROW],
                                    same[:, (q % 2) * Q + s, :], picked[:, (q % 2) * Q + s, :], start=True, stop=True)
                ins.then_inc(equals_summed, 1)

            def back_round(i, first, last):
                _, at = nc.values_load_multi_w_load_instructions(
                    off_row[0:1, bass.ds(i * RING, RING)], engines=[mybir.EngineType.PE], min_val=0,
                    max_val=(BLOCKS - 1) * D,
                    skip_runtime_bounds_check_because="the blocks are clamped where the offsets are made")
                for q in range(GI):
                    if q or not first:
                        sum_equals(i if q else i - 1, (q - 1) % GI)
                    if q < GI - 1 or not last:
                        spread_group(i if q < GI - 1 else i + 1, (q + 1) % GI)
                    pick_rows(i, q, at)

            spread_group(0, 0)
            back_round(0, True, False)
            with pe.Fori(1, ITERS - 1) as i:
                back_round(i, False, False)
            back_round(ITERS - 1, False, True)
            sum_equals(ITERS - 1, GI - 1)
            pe.wait_ge(mean_ready, 1)
            for q in range(ceil_div(BLOCKS, 4)):
                k = min(4, BLOCKS - 4 * q)
                if q >= 4:
                    pe.wait_ge(mean_stored, q - 3)
                for j in range(k):
                    ins = pe.transpose(PS[:, q % 4, j * P:(j + 1) * P], acc_m[:, 4 * q + j, 0:D], ident[:, :])
                ins.then_inc(mean_turned, 1)
            for q in range(ceil_div(BLOCKS, 4)):
                k = min(4, BLOCKS - 4 * q)
                pe.wait_ge(mean_stored, q + 1)
                if q >= 4:
                    pe.wait_ge(mean_added, q - 3)
                for j in range(k):
                    b = 4 * q + j
                    to = PS[:, 4 + q % 4, j * P:(j + 1) * P]
                    pe.matmul(to, hT[:, b * P:(b + 1) * P], w_mean[:, 0, :], start=True, stop=False)
                    ins = pe.matmul(to, msg[:, b * P:(b + 1) * P], w_mean[:, 1, :], start=False, stop=True)
                ins.then_inc(mean_summed, 1)
            pe.wait_ge(mean_added, ceil_div(BLOCKS, 4))
            turn_h(2)
            edge_sums(1)
            for q in range(ceil_div(BLOCKS, 4)):
                if q >= 8:
                    pe.wait_ge(types_stored, q - 7)
                k = min(4, BLOCKS - 4 * q)
                for j in range(k):
                    ins = pe.transpose(PS[0:TYPES, q % 8, j * P:(j + 1) * P], types_at[:, 4 * q + j, :], ident[:, :])
                ins.then_inc(types_turned, 1)
            pe.wait_ge(types_stored, ceil_div(BLOCKS, 4))
            for q in range(ceil_div(NPAD, 512)):
                w = min(512, NPAD - 512 * q)
                if q >= 2:
                    pe.wait_ge(msg_stored, q - 1)
                pe.matmul(PS[:, q % 2, 0:w], wT[:, 0, :], acc_d[:, q * 512:q * 512 + w], start=True, stop=False)
                pe.matmul(PS[:, q % 2, 0:w], emb_b[:, :], typesT[:, q * 512:q * 512 + w], start=False, stop=True
                          ).then_inc(msg_summed, 1)
            pe.wait_ge(msg_stored, ceil_div(NPAD, 512))

            def turn_gru(q):
                k = min(QW, NPAD - QW * q) // P
                pe.wait_ge(gru_ready, q + 1)
                if q >= 2:
                    pe.wait_ge(gru_added, q - 1)
                for j in range(k):
                    ins = pe.transpose(PS[:, q % 2, j * P:(j + 1) * P], gate[:, q % 2, 3, j * P:(j + 1) * P], ident[:, :])
                ins.then_inc(gru_turned, 1)

            for q in range(NQ):
                w = min(QW, NPAD - QW * q)
                pr = 2 + 2 * (q % 2)
                if q >= 2:
                    pe.wait_ge(rz_ready, 2 * (q - 1))
                    pe.wait_ge(n_summed, q - 1)
                m, hh = msg[:, q * QW:q * QW + w], hT[:, q * QW:q * QW + w]
                for g in range(2):
                    pe.matmul(PS[:, pr, g * QW:g * QW + w], wT[:, 1 + g, :], m, start=True, stop=False)
                    pe.matmul(PS[:, pr, g * QW:g * QW + w], wT[:, 4 + g, :], hh, start=False, stop=True)
                pe.matmul(PS[:, pr + 1, 0:w], wT[:, 3, :], m, start=True, stop=True)
                pe.matmul(PS[:, pr + 1, QW:QW + w], wT[:, 6, :], hh, start=True, stop=True).then_inc(gates_summed, 1)
                if q >= 1:
                    turn_gru(q - 1)
            turn_gru(NQ - 1)
            pe.wait_ge(gru_added, NQ)
            turn_h(3)
            for q in range(ceil_div(BLOCKS, 3)):
                k = min(3, BLOCKS - 3 * q)
                if q >= 8:
                    pe.wait_ge(att_stored, q - 7)
                for j in range(k):
                    b = 3 * q + j
                    ins = pe.matmul(PS[:, q % 8, j * ROW3:(j + 1) * ROW3], hT[:, b * P:(b + 1) * P], w3[:, :],
                                    start=True, stop=True)
                ins.then_inc(att_summed, 1)
            pe.wait_ge(att_stored, NATT)

            def spread_low(i, g):
                pe.wait_ge(lows_loaded[(g // 2) % 2], i * (16 * GROUPS3 // 4) + 16 * (g // 4 + 1))
                if not (isinstance(i, int) and i == 0 and g < 2):
                    pe.wait_ge(low_apart, i * GROUPS3 + (g - 1))
                pe.matmul(PS[:, g % 2, :], ones_row, lows[:, (g // 2) % 2, (g % 2) * G3:(g % 2 + 1) * G3, :].rearrange("p s e -> p (s e)"),
                          start=True, stop=True).then_inc(low_spread, 1)

            def pick_logits(i, g):
                pe.wait_ge(low_hot, i * GROUPS3 + (g + 1))
                if not (isinstance(i, int) and i == 0 and g < 2):
                    pe.wait_ge(multiplied3, i * GROUPS3 + (g - 1))
                for s in range(G3):
                    for a in range(3):
                        ins = pe.matmul(PS[:, 2 + 2 * (g % 2) + s // 2, (s % 2) * 256:(s % 2) * 256 + HB],
                                        low_hots[:, g % 2, s * P:(s + 1) * P], parts3[:, a, :], start=(a == 0), stop=(a == 2))
                ins.then_inc(picked3, 1)

            def pick_round(i, last):
                for g in range(GROUPS3):
                    if g < GROUPS3 - 1:
                        spread_low(i, g + 1)
                    elif not last:
                        spread_low(i + 1, 0)
                    pick_logits(i, g)

            pe.wait_ge(parts3_ready, 1)
            spread_low(0, 0)
            pick_round(0, False)
            with pe.Fori(1, IT3 - 1) as i:
                pick_round(i, False)
            pick_round(IT3 - 1, True)
            pe.wait_ge(ends_turn, 1)
            pe.transpose(PS[0:HEADS, 0, 0:P], row_ends[:, 0:HEADS], ident[:, :])
            pe.transpose(PS[0:HEADS, 0, P:2 * P], row_ends[:, HEADS:2 * HEADS], ident[:, :]).then_inc(turned3, 1)
            pe.wait_ge(carry_row, 1)
            pe.transpose(PS[:, 1, 0:HEADS], rowT[:, 2, :], ident[0:HEADS, 0:HEADS]).then_inc(turned3, 1)
            pe.wait_ge(ends_turn, 2)
            pe.transpose(PS[0:HEADS, 2, 0:P], row_ends[:, 2 * HEADS:3 * HEADS], ident[:, :]).then_inc(turned3, 1)
            pe.wait_ge(carry_row, 2)
            pe.transpose(PS[:, 3, 0:HEADS], rowT[:, 7, :], ident[0:HEADS, 0:HEADS]).then_inc(turned3, 1)

        @block.vector
        def _(dve):
            steps_of_dve = [0]

            def link(ins):
                steps_of_dve[0] += 1
                ins.then_inc(dve_done, 1)
                dve.wait_ge(dve_done, steps_of_dve[0])

            dve.wait_ge(consts_set, 2)
            dve.memset(flat_ring[:, 0:KW], 0.0).then_inc(ring_cleared, 1)
            dve.memset(ones[:, :], 1.0)
            dve.tensor_scalar(minus_p[:, :], pidx[:, :], -1.0, None, ALU.mult)
            dve.memset(one13[:, :], 1.0)
            dve.memset(vw[:, :, :], 1.0)
            dve.tensor_scalar(ident[:, :], iota_k[:, 0:P], pidx[:, 0:1], None, ALU.is_equal)
            dve.tensor_scalar(tri[:, :], iota_k[:, 0:P], pidx[:, 0:1], None, ALU.is_ge)
            link(dve.tensor_scalar(pad_start[:, :], pidx[:, :], float(CREST), 1.0e6, ALU.is_ge, ALU.mult))
            dve.wait_ge(src3_loaded, 32)
            link(dve.tensor_scalar(low_i, raw3, P - 1, None, ALU.bitwise_and))
            dve.tensor_copy(flat_ring[:, 0:KW], low_i).then_inc(low_made, 1)
            dve.wait_ge(ends_loaded, 80)
            dve.tensor_scalar(dump[:, :], pidx[:, :], float(NPAD), None, ALU.add)
            dve.tensor_scalar(pick[:, 0, :], ones[0:3, :], pidx[0:3, 0:1], 2.0, ALU.mult, ALU.is_equal)
            dve.tensor_scalar(pick[:, 1, :], ones[0:3, :], pidx[0:3, 0:1], 2.0, ALU.mult, ALU.is_lt)
            shift = P.bit_length() - 1
            dve.tensor_scalar(fb_i[:, :], first_dst[:, :], shift, None, ALU.arith_shift_right)
            link(dve.tensor_scalar(pb_i[:, :], prev_dst[:, :], shift, None, ALU.arith_shift_right))
            dve.tensor_copy(fb[:, :], fb_i[:, :])
            link(dve.tensor_copy(pb[:, :], pb_i[:, :]))
            link(dve.scalar_tensor_tensor(out=adv[:, :], in0=fb[:, :], scalar=-1.0, in1=pb[:, :], op0=ALU.add, op1=ALU.subtract))
            dve.tensor_copy(vw[:, :, 1], adv[:, :])
            link(dve.tensor_tensor_scan(adv_sum[:, :], one13[:, 0:CT], adv[:, :], 0.0, ALU.mult, ALU.add))
            dve.tensor_tensor(adv_sum[:, :], adv_sum[:, :], adv[:, :], ALU.subtract).then_inc(adv_ready, 1)
            dve.wait_ge(adv_summed, 1)
            link(dve.tensor_tensor(start_step[:, :], fb[:, :], PS[:, 0, 0:CT], ALU.subtract))
            link(dve.tensor_tensor(start_step[:, CT - 1:CT], start_step[:, CT - 1:CT], pad_start[:, :], ALU.add))
            for t in range(CT):
                ins = dve.tensor_scalar(marks[:, t, :], iota_k[:, :], start_step[:, t:t + 1], None, ALU.is_ge)
            ins.then_inc(steps_marked, 1)
            dve.wait_ge(steps_summed, 1)
            pairs = PS[:, 1, 0:2 * KT].rearrange("p (k a) -> p k a", a=2)
            dve.tensor_scalar(chunk_idx[:, :], pairs[:, :, 0], -1.0, None, ALU.add).then_inc(chunks_known, 1)
            link(dve.tensor_tensor(blk[:, :], pairs[:, :, 1], kcol[:, :], ALU.add))
            dve.tensor_scalar(neg_base[:, :], blk[:, :], -float(P), None, ALU.mult)
            flat = PS[0:1, 2:6, 0:KW // 4]
            link(dve.tensor_tensor(brow[:, :].rearrange("p (a b) -> p a b", a=4), flat,
                                   iota_k[0:1, :].rearrange("p (a b) -> p a b", a=4), ALU.add))
            link(dve.tensor_scalar(brow[:, :], brow[:, :], float(BLOCKS - 1), 0.0, ALU.min, ALU.max))
            dve.tensor_scalar(off_row[:, :], brow[:, :], float(ROW), None, ALU.mult).then_inc(chunks_known, 1)
            dve.wait_ge(chunks_known, 2)
            dve.memset(msg, 0.0).then_inc(zeros_ready, 1)

            def layer_norm(n):
                def moments(g):
                    b0 = g * LNG
                    for b in range(b0, b0 + LNG):
                        ins = dve.bn_stats(stats[:, b, :], X[:, b, :])
                    link(ins)
                    for b in range(b0, b0 + LNG):
                        ins = dve.bn_aggr(mv[:, b, :], stats[:, b, :])
                    link(ins)
                    dve.tensor_scalar(ve[:, b0:b0 + LNG], mv[:, b0:b0 + LNG, 1], EPS, None, ALU.add).then_inc(ln_var, 1)

                def scales(g):
                    b0 = g * LNG
                    dve.wait_ge(ln_sd, NLN * n + g + 1)
                    link(dve.reciprocal(rstd[:, b0:b0 + LNG], sd[:, b0:b0 + LNG]))
                    dve.scalar_tensor_tensor(out=nmr[:, b0:b0 + LNG], in0=mv[:, b0:b0 + LNG, 0], scalar=-1.0,
                                             in1=rstd[:, b0:b0 + LNG], op0=ALU.mult, op1=ALU.mult).then_inc(ln_scale, 1)

                if n:
                    dve.wait_ge(ln_relu, NLN * n)
                for g in range(NLN):
                    moments(g)
                    if g:
                        scales(g - 1)
                scales(NLN - 1)

            dve.wait_ge(x_loaded, 32)
            layer_norm(0)
            dve.wait_ge(rows_gathered[0], 16 * KT)
            for t in range(KT):
                ins = dve.tensor_scalar(rows[0][:, t * P:(t + 1) * P], rows_i[0][:, t * P:(t + 1) * P], neg_base[:, t:t + 1],
                                        None, ALU.add)
            ins.then_inc(rows_ready[0], 1)
            dve.wait_ge(rows_gathered[2], 16 * KT)
            dve.wait_ge(rows_gathered[1], 16 * KT)
            dve.tensor_scalar(src_high, rows_i[1], -P, None, ALU.bitwise_and)
            link(dve.tensor_scalar(src_low, rows_i[1], P - 1, None, ALU.bitwise_and))
            dve.tensor_copy(rows3_bf[:, 0, :], src_high)
            dve.tensor_copy(rows3_bf[:, 1, :], src_low)
            dve.tensor_scalar(rows3_bf[:, 2, :], rows[0], -1.0, OUTSIDE, ALU.max, ALU.min).then_inc(parts_made, 1)
            dve.tensor_scalar(rows[2], rows_i[2], 0.0, float(TYPES - 1), ALU.max, ALU.min).then_inc(rows_ready[2], 1)
            dve.wait_ge(rows_turned, 4)
            link(dve.memset(acc[:, :], 0.0))

            def edge_adds(turn):
                width = (ROW, D)[turn]

                def hots(i, h):
                    k = bass.ds(i * RING + h * HALF, HALF)
                    us = slice(h * HALF, (h + 1) * HALF)
                    lane = iota_k[:, 0:P].unsqueeze(1).broadcast_to([P, HALF, P])
                    rel = dst_rel[:, k].unsqueeze(2).broadcast_to([P, HALF, P])
                    ins = dve.tensor_tensor(onehot[:, us, :], lane, rel, ALU.is_equal)
                    if turn == 0:
                        kinds = iota_k[:, 0:TYPES].unsqueeze(1).broadcast_to([P, HALF, TYPES])
                        kind = type_step[:, k].unsqueeze(2).broadcast_to([P, HALF, TYPES])
                        ins = dve.tensor_tensor(ring[:, us, D:ROW], kinds, kind, ALU.is_equal)
                    ins.then_inc(hot_ready, 1)

                def adds(i, h, at):
                    for s in range(HALF):
                        u = h * HALF + s
                        if u % 2 == 0:
                            dve.wait_ge(summed, i * RING + (STEPS * turn + u + 2))
                        dve.wait_ge(added, i * RING + (STEPS * turn + u))
                        a = acc[:, bass.ds(at[u], width)]
                        dve.tensor_tensor(a, a, slot(u, width), ALU.add).then_inc(added, 1)

                def body(i, more):
                    _, at = nc.values_load_multi_w_load_instructions(
                        off_row[0:1, bass.ds(i * RING, RING)], engines=[DVE_ENGINE], min_val=0,
                        max_val=(BLOCKS - 1) * width,
                        skip_runtime_bounds_check_because="the blocks are clamped where the offsets are made")
                    hots(i, 1)
                    adds(i, 0, at)
                    if more:
                        hots(i + 1, 0)
                    adds(i, 1, at)

                hots(0, 0)
                with dve.Fori(0, ITERS - 1) as i:
                    body(i, True)
                body(ITERS - 1, False)
                dve.wait_ge(added, STEPS * (turn + 1))

            dve.wait_ge(rows_stored, 4)
            dve.wait_ge(low_turned, 1)
            dve.wait_ge(low_stored, 16)
            edge_adds(0)

            link(dve.tensor_scalar(off_row[:, :], brow[:, :], float(D), None, ALU.mult))
            acc_r = acc[:, :].rearrange("p (b r) -> p b r", r=ROW)
            dve.tensor_copy(types_at[:, :, :], acc_r[:, :, D:ROW])
            link(dve.tensor_reduce(degree[:, :], acc_r[:, :, D:ROW], AX, ALU.add))
            dve.tensor_tensor(X[:, :, :], X[:, :, :], acc_r[:, :, 0:D], ALU.add).then_inc(degree_ready, 1)
            dve.wait_ge(degree_ready, 1)
            link(dve.tensor_scalar(in_block[:, :], dst_rel[:, :], float(P), None, ALU.is_lt))
            link(dve.scalar_tensor_tensor(out=in_block[:, :], in0=dst_rel[:, :], scalar=0.0, in1=in_block[:, :],
                                          op0=ALU.is_ge, op1=ALU.mult))
            dve.wait_ge(nodes_summed, 1)
            link(dve.tensor_copy(total[:, :], PS[:, 1, 0:BLOCKS]))
            link(dve.tensor_tensor_scan(before[:, :], one13[:, :], total[:, :], 0.0, ALU.mult, ALU.add))
            link(dve.tensor_tensor(before[:, :], before[:, :], total[:, :], ALU.subtract))
            dve.tensor_scalar(empty[:, :], degree[:, :], 0.0, float(NOBODY), ALU.is_equal, ALU.mult)
            link(dve.tensor_tensor(upto[:, :], before[:, :], PS[:, 0, 0:BLOCKS], ALU.add))
            link(dve.tensor_tensor(upto[:, :], upto[:, :], empty[:, :], ALU.add))
            dve.tensor_tensor(begin_i[:, :], upto[:, :], degree[:, :], ALU.subtract)
            dve.tensor_scalar(end_i[:, :], upto[:, :], -1.0, None, ALU.add).then_inc(nodes_counted, 1)
            dve.wait_ge(w_loaded, WL)
            dve.tensor_tensor(emb_b[:, :], emb_b[:, :], emb[:, :], ALU.add)
            dve.tensor_tensor(brz[:, :], bcol[:, 0:2], bcol[:, 3:5], ALU.add)
            dve.wait_ge(att_folded, 1)
            dve.tensor_copy(w3[:, D:ROW3], PS[:, 4, 0:HA]).then_inc(w3_ready, 1)

            layer_norm(1)
            dve.wait_ge(h_stored, ceil_div(BLOCKS, 4))

            GI = RING // Q

            def mark(i, q):
                gs = slice((q % 2) * Q, (q % 2 + 1) * Q)
                k = bass.ds(i * RING + q * Q, Q)
                done = i * GI + (q + 1)
                dve.wait_ge(spread, done)
                quad = lambda bank: PS[:, bank, :].rearrange("p (s e) -> p s e", s=Q)
                dve.tensor_scalar(dstT[:, gs, :], quad(0), pidx[:, 0:1], None, ALU.is_equal).then_inc(picks_ready, 1)
                dve.tensor_tensor(same[:, gs, :], quad(1), src_idx[:, k].unsqueeze(2).broadcast_to([P, Q, P]), ALU.is_equal
                                  ).then_inc(same_raw, 1)
                dve.tensor_scalar(src_less[:, q * Q:(q + 1) * Q], src_idx[:, k], dump[:, 0:1], None, ALU.subtract
                                  ).then_inc(less_ready, 1)
                dve.wait_ge(same_raw, done)
                dve.tensor_tensor(same[:, gs, :], same[:, gs, :], tri[:, :].unsqueeze(1).broadcast_to([P, Q, P]), ALU.mult
                                  ).then_inc(same_ready, 1)
                dve.wait_ge(same_ready, done)
                dve.tensor_reduce(equals[:, q * Q:(q + 1) * Q], same[:, gs, :], AX, ALU.add).then_inc(equals_ready, 1)
                dve.wait_ge(equals_ready, done)
                dve.wait_ge(less_ready, done)
                dve.scalar_tensor_tensor(out=last_src[:, q * Q:(q + 1) * Q], in0=equals[:, q * Q:(q + 1) * Q], scalar=1.0,
                                         in1=src_less[:, q * Q:(q + 1) * Q], op0=ALU.is_equal, op1=ALU.mult
                                         ).then_inc(void_marked, 1)
                dve.wait_ge(void_marked, done)
                for s in range(Q):
                    u = q * Q + s
                    if not (isinstance(i, int) and i == 0):
                        dve.wait_ge(scattered[u % COPIES], i * 32 + (16 * (u // COPIES) - 16))
                dve.tensor_scalar(idx_stage[:, q * Q:(q + 1) * Q], last_src[:, q * Q:(q + 1) * Q], dump[:, 0:1], None, ALU.add
                                  ).then_inc(places_ready, 1)

            for q in range(GI):
                mark(0, q)
            with dve.Fori(1, ITERS) as i:
                for q in range(GI):
                    mark(i, q)

            for c in range(PIECES):
                b0, nb = c * PIECE, min(PIECE, BLOCKS - c * PIECE)
                dve.wait_ge(pieces_loaded[c % 2], 16 * COPIES * (c // 2 + 1))
                dve.tensor_reduce(acc[:, b0 * MROW:(b0 + nb) * MROW],
                                  pieces[c % 2][:, 0:COPIES * nb * MROW].rearrange("p (n m) -> p m n", n=COPIES), AX, ALU.add
                                  ).then_inc(piece_added, 1)
            dve.wait_ge(piece_added, PIECES)
            link(dve.tensor_scalar(rcount[:, :], acc_m[:, :, D], 1.0, None, ALU.max))
            link(dve.reciprocal(rcount[:, :], rcount[:, :]))
            dve.tensor_tensor(acc_m[:, :, 0:D], acc_m[:, :, 0:D], rcount[:, :].unsqueeze(2).broadcast_to([P, BLOCKS, D]),
                              ALU.mult).then_inc(mean_ready, 1)
            link(dve.tensor_tensor(X[:, :, :], X[:, :, :], b_mean[:, :].unsqueeze(1).broadcast_to([P, BLOCKS, D]), ALU.add))
            for q in range(ceil_div(BLOCKS, 4)):
                k = min(4, BLOCKS - 4 * q)
                dve.wait_ge(mean_summed, q + 1)
                xs = X[:, 4 * q:4 * q + k, :].rearrange("p b f -> p (b f)")
                dve.tensor_tensor(xs, xs, PS[:, 4 + q % 4, 0:k * P], ALU.add).then_inc(mean_added, 1)
            link(dve.memset(acc[:, 0:NPAD], 0.0))
            dve.wait_ge(mean_added, ceil_div(BLOCKS, 4))
            layer_norm(2)
            dve.wait_ge(h_stored, 2 * ceil_div(BLOCKS, 4))
            edge_adds(1)

            dve.memset(sumsN[:, :, :], 0.0)
            dve.wait_ge(last_loaded, 80)
            link(dve.tensor_tensor(not_start, dst3, prev3, ALU.is_equal))
            link(dve.memset(not_start[0:1, 0:1], 0.0))
            link(dve.tensor_scalar(start_low, not_start, -1.0, BIG, ALU.add, ALU.mult))
            dve.tensor_reduce(row_ends[:, HEADS:HEADS + 1], start_low, AX, ALU.min)
            link(dve.tensor_scalar(src3[:, 0:ONEHOT_COLS], src3[:, 0:ONEHOT_COLS], shift, None, ALU.arith_shift_right))
            dve.memset(ones_row, 1.0)

            def gru_add(q):
                k = min(QW, NPAD - QW * q) // P
                dve.wait_ge(gru_turned, q + 1)
                dve.tensor_tensor(X[:, 2 * q:2 * q + k, :].rearrange("p b f -> p (b f)"),
                                  X[:, 2 * q:2 * q + k, :].rearrange("p b f -> p (b f)"), PS[:, q % 2, 0:k * P], ALU.add
                                  ).then_inc(gru_added, 1)

            for q in range(NQ):
                w = min(QW, NPAD - QW * q)
                pr = 2 + 2 * (q % 2)
                r, z, n, t = (gate[:, q % 2, a, 0:w] for a in range(4))
                dve.wait_ge(rz_ready, 2 * q + 2)
                if q >= 2:
                    dve.wait_ge(gru_turned, q - 1)
                link(dve.scalar_tensor_tensor(out=t, in0=PS[:, pr + 1, QW:QW + w], scalar=bcol[:, 5:6], in1=r,
                                              op0=ALU.add, op1=ALU.mult))
                dve.tensor_tensor(t, t, PS[:, pr + 1, 0:w], ALU.add).then_inc(n_summed, 1)
                if q >= 1:
                    gru_add(q - 1)
                dve.wait_ge(n_ready, q + 1)
                link(dve.tensor_tensor(t, hT[:, q * QW:q * QW + w], n, ALU.subtract))
                link(dve.tensor_tensor(t, t, z, ALU.mult))
                dve.tensor_tensor(t, t, n, ALU.add).then_inc(gru_ready, 1)
            gru_add(NQ - 1)
            dve.wait_ge(gru_added, NQ)
            layer_norm(3)


            dve.wait_ge(att_stored, NATT)
            own = HWv[:, :, D:D + HEADS].rearrange("p b h -> p h b")
            part = lambda a: parts3[:, a, :].rearrange("p (h b) -> p h b", h=HEADS)
            left = left3.rearrange("p (h b) -> p h b", h=HEADS)
            link(dve.tensor_copy(part(0), own))
            link(dve.tensor_tensor(left, own, part(0), ALU.subtract))
            link(dve.tensor_copy(part(1), left))
            link(dve.tensor_tensor(left, left, part(1), ALU.subtract))
            dve.tensor_copy(part(2), left).then_inc(parts3_ready, 1)
            dve.wait_ge(parts3_ready, 1)

            def high_hots3(i, m):
                dve.tensor_tensor(highs[:, m % 2, :, :], iota_k[:, 0:BLOCKS].unsqueeze(1).broadcast_to([P, 2 * G3, BLOCKS]),
                                  src3[:, bass.ds(i * COLS3 + m * 2 * G3, 2 * G3)].unsqueeze(2).broadcast_to([P, 2 * G3, BLOCKS]),
                                  ALU.is_equal).then_inc(high_hot, 1)

            def take_logits(i, last):
                M3 = GROUPS3 // 2
                for m in range(M3):
                    dve.wait_ge(high_hot, i * M3 + (m + 1))
                    for v in range(2):
                        g = 2 * m + v
                        dve.wait_ge(picked3, i * GROUPS3 + (g + 1))
                        dve.tensor_tensor(
                            products[:, m % 2, v * G3:(v + 1) * G3, :].rearrange("p s (h b) -> p s h b", h=HEADS),
                            PS[:, 2 + 2 * (g % 2):4 + 2 * (g % 2), :].rearrange("p c (s m) -> p (c s) m", s=2)[:, :, 0:HB].rearrange(
                                "p s (h b) -> p s h b", h=HEADS),
                            highs[:, m % 2, v * G3:(v + 1) * G3, :].unsqueeze(2).broadcast_to([P, G3, HEADS, BLOCKS]),
                            ALU.mult).then_inc(multiplied3, 1)
                    if m < M3 - 1:
                        high_hots3(i, m + 1)
                    elif not last:
                        high_hots3(i + 1, 0)
                    dve.wait_ge(multiplied3, i * GROUPS3 + (2 * m + 2))
                    dve.tensor_reduce(al3[:, bass.ds(i * COLS3 + m * 2 * G3, 2 * G3), :],
                                      products[:, m % 2, :, :].rearrange("p s (h b) -> p s h b", h=HEADS), AX, ALU.add
                                      ).then_inc(picked_logits, 1)

            high_hots3(0, 0)
            with dve.Fori(0, IT3 - 1) as i:
                take_logits(i, False)
            take_logits(IT3 - 1, True)
            dve.wait_ge(picked_logits, IT3 * GROUPS3 // 2)
            dve.wait_ge(first_back, 16)
            dve.wait_ge(filled_back, 16)
            for h in range(HEADS):
                ins = dve.tensor_tensor_scan(aj3[:, :, h], not_start, aj3[:, :, h], first_logits[:, HEADS + h:HEADS + h + 1],
                                             ALU.mult, ALU.add)
            link(ins)
            dve.wait_ge(all_logits, (ROUNDS3 - 1) * (RING // G3) + ceil_div(TAIL3, G3))
            a = al[:, 0:AN]
            link(dve.tensor_tensor(a, a, aj, ALU.add))
            link(dve.scalar_tensor_tensor(out=a, in0=a, scalar=0.2, in1=a, op0=ALU.mult, op1=ALU.max))
            for h in range(HEADS):
                ins = dve.tensor_tensor_scan(mx3[:, :, h], start_low, al3[:, 0:CHUNKS, h], -BIG, ALU.add, ALU.max)
            link(ins)
            dve.tensor_copy(row_ends[:, 0:HEADS], mx3[:, CHUNKS - 1, :])
            for h in range(1, HEADS):
                dve.tensor_copy(row_ends[:, HEADS + h:HEADS + h + 1], row_ends[:, HEADS:HEADS + 1])
            dve.tensor_copy(carry[:, 0:1], pidx[:, :]).then_inc(ends_turn, 1)
            dve.wait_ge(turned3, 1)
            link(dve.tensor_copy(rowT[:, 0:2, :].rearrange("p a b -> p (a b)"), PS[0:HEADS, 0, 0:2 * P]))
            dve.memset(rowT[:, 2, 0:1], -BIG)
            link(dve.tensor_tensor_scan(rowT[:, 3, :], rowT[:, 1, :], rowT[:, 0, :], -BIG, ALU.add, ALU.max))
            dve.tensor_copy(rowT[:, 2, 1:P], rowT[:, 3, 0:P - 1]).then_inc(carry_row, 1)
            dve.wait_ge(turned3, 2)
            link(dve.tensor_copy(carry[:, 0:HEADS], PS[:, 1, 0:HEADS]))
            for h in range(HEADS):
                ins = dve.tensor_tensor_scan(mx3[:, :, h], start_low, al3[:, 0:CHUNKS, h], carry[:, h:h + 1], ALU.add, ALU.max)
            link(ins)
            link(dve.tensor_tensor(aj[:, HEADS:AN], mx[:, 0:AN - HEADS], mx[:, HEADS:AN], ALU.subtract))
            link(dve.tensor_tensor(aj[:, 0:HEADS], carry[:, 0:HEADS], mx[:, 0:HEADS], ALU.subtract))
            dve.tensor_tensor(aj3, aj3, start_low.unsqueeze(2).broadcast_to([P, CHUNKS, HEADS]), ALU.add).then_inc(exp_in, 1)
            dve.tensor_tensor(a, a, mx, ALU.subtract).then_inc(exp_in, 1)
            link(dve.tensor_tensor(rowT[:, 5, :], rowT[:, 2, :], rowT[:, 3, :], ALU.subtract))
            dve.tensor_tensor(rowT[:, 5, :], rowT[:, 5, :], rowT[:, 1, :], ALU.add).then_inc(exp_in, 1)
            dve.wait_ge(exp_out, 3)
            for h in range(HEADS):
                ins = dve.tensor_tensor_scan(mx3[:, :, h], aj3[:, :, h], al3[:, 0:CHUNKS, h], 0.0, ALU.mult, ALU.add)
            link(ins)
            dve.tensor_copy(row_ends[:, 2 * HEADS:3 * HEADS], mx3[:, CHUNKS - 1, :]).then_inc(ends_turn, 1)
            dve.wait_ge(turned3, 3)
            link(dve.tensor_copy(rowT[:, 4, :], PS[0:HEADS, 2, 0:P]))
            dve.memset(rowT[:, 7, 0:1], 0.0)
            link(dve.tensor_tensor_scan(rowT[:, 6, :], rowT[:, 5, :], rowT[:, 4, :], 0.0, ALU.mult, ALU.add))
            dve.tensor_copy(rowT[:, 7, 1:P], rowT[:, 6, 0:P - 1]).then_inc(carry_row, 1)
            dve.wait_ge(turned3, 4)
            link(dve.tensor_copy(carry[:, HEADS:2 * HEADS], PS[:, 3, 0:HEADS]))
            for h in range(HEADS):
                ins = dve.tensor_tensor_scan(mx3[:, :, h], aj3[:, :, h], al3[:, 0:CHUNKS, h], carry[:, HEADS + h:HEADS + h + 1],
                                             ALU.mult, ALU.add)
            ins.then_inc(sums_ready, 1)
            dve.wait_ge(sums_back, 16 * BLOCKS)
            link(dve.tensor_scalar(ratio[:, :, :], sumsN[:, :, :], 1e-16, None, ALU.add))
            link(dve.reciprocal(ratio[:, :, :], ratio[:, :, :]))
            link(dve.tensor_tensor(ratio[:, :, :], ratio[:, :, :], sumsN[:, :, :], ALU.mult))
            for h in range(HEADS):
                cols = slice(h * C, (h + 1) * C)
                ins = dve.tensor_tensor(HWv[:, :, cols], HWv[:, :, cols],
                                        ratio[:, :, h].unsqueeze(2).broadcast_to([P, BLOCKS, C]), ALU.mult)
            link(ins)
            dve.tensor_tensor(X[:, :, :], X[:, :, :], HWv[:, :, 0:D], ALU.add).then_inc(out_ready, 1)


_NAMES = ["x", "src", "dst", "edge_type_9", "edge_weight1", "L1_gnn_W", "L1_gnn_b", "L2_gnn_W_msg", "L2_gnn_b_msg",
          "L2_gnn_edge_embed", "L2_gnn_W_ih", "L2_gnn_W_hh", "L2_gnn_b_ih", "L2_gnn_b_hh", "L3_gnn_weight", "L3_gnn_att"]


def kernel(**inputs):
    import numpy as np
    import concourse.bacc as bacc
    from concourse.bass_utils import run_bass_kernel_spmd as run

    nc = bacc.Bacc("TRN2", target_bir_lowering=False, num_devices=1)
    arrays, args = {}, []
    for name in _NAMES:
        a = np.ascontiguousarray(inputs[name])
        if name == "edge_weight1":
            a = a.reshape(-1)
        arrays[f"in_{name}"] = a
        args.append(nc.dram_tensor(f"in_{name}", a.shape, mybir.dt.from_np(a.dtype), kind="ExternalInput").ap())
    out = nc.dram_tensor("out", inputs["x"].shape, F32, kind="ExternalOutput").ap()
    build(nc, *args, out)
    return run(nc, [arrays], core_ids=[0]).results[0]["out"]
```

```python
from contextlib import ExitStack

import concourse.bass as bass
from concourse import mybir
from concourse.alu_op_type import AluOpType as ALU

ACT = mybir.ActivationFunctionType
F32 = mybir.dt.float32
BF16 = mybir.dt.bfloat16
I32 = mybir.dt.int32
AX = mybir.AxisListType.X
DVE_ENGINE = mybir.EngineType.DVE


def ceil_div(a, b):
    return -(-a // b)


def build(nc, x, src, dst, edge_type, edge_weight, mean_w, mean_b, msg_w, msg_b, embed, w_ih, w_hh,
          b_ih, b_hh, att_w, att, out):
    P = 128
    NODES, D = x.shape
    (EDGES,) = src.shape
    BLOCKS = ceil_div(NODES, P)
    LAST = NODES - (BLOCKS - 1) * P
    NPAD = BLOCKS * P
    CHUNKS = ceil_div(EDGES, P)
    EPAD = CHUNKS * P
    TAIL = EPAD - EDGES
    RING = 16
    HALF = RING // 2
    ITERS = ceil_div(CHUNKS + BLOCKS - 1, RING)
    STEPS = ITERS * RING
    CT = ceil_div(CHUNKS, P)
    CREST = CHUNKS - (CT - 1) * P
    KT = ceil_div(STEPS, P)
    KW = KT * P
    TYPES = embed.shape[0]
    ROW = D + TYPES
    NOBODY = 1 << 20
    EPS = 1e-5
    HEADS = att.shape[1]
    C = att.shape[2] // 2
    HA = 2 * HEADS
    ROW3 = D + HA
    BIG = 1.0e38
    IT3 = 37
    COLS3 = 2 * RING
    ONEHOT_COLS = IT3 * COLS3
    GATHER_COLS = CHUNKS - ONEHOT_COLS
    QUARTER = 3
    RING3 = 4 * QUARTER
    ROUNDS3 = ceil_div(GATHER_COLS, RING3)
    TAIL3 = GATHER_COLS - (ROUNDS3 - 1) * RING3
    LATE3 = 5
    G3 = 4
    GROUPS3 = COLS3 // G3
    LOWS = 2 * P
    HIGHS = ceil_div(BLOCKS, 2)
    HM = HEADS * HIGHS
    LNG = 6
    NLN = ceil_div(BLOCKS, LNG)
    COPIES = 8
    MROW = D + 1
    Q = 4
    PIECE = LNG // 2
    PIECES = ceil_div(BLOCKS, PIECE)
    OUTSIDE = 200.0
    QW = 256
    NQ = ceil_div(NPAD, QW)
    NATT = ceil_div(BLOCKS, 3)
    FINAL = 7
    FB = BLOCKS // FINAL
    WL = 16 * (11 + 2 * HEADS)
    assert D == P and BLOCKS % FINAL == 0 and KT == CT and LATE3 + ROUNDS3 <= IT3 and TAIL3 > 0

    ctx = ExitStack()
    with ctx:
        def sb(name, shape, dt=F32):
            return ctx.enter_context(nc.sbuf_tensor(name, shape, dt))

        def sem(name):
            return ctx.enter_context(nc.semaphore(name))

        def dram(name, shape, dt=F32):
            return nc.dram_tensor(name, shape, dt).ap()

        dst_pad = dram("dst_pad", (EPAD,), I32)
        src_pad = dram("src_pad", (EPAD,), I32)
        type_pad = dram("type_pad", (EPAD,), I32)
        weight_pad = dram("weight_pad", (EPAD,), F32)
        tables = [dram(f"table{n}", (NPAD, D)) for n in range(2)]
        edge_rows = dram("edge_rows", (KW, 3, P), BF16)
        back = [dram(f"back{n}", (NPAD + P, MROW)) for n in range(COPIES)]
        low_rows = dram("low_rows", (KW, P), BF16)
        logit_table = dram("logit_table", (NPAD, HA))
        start_logits = dram("start_logits", (EPAD, HEADS))
        sums_dram = dram("sums_dram", (EPAD, HEADS))

        X = sb("X", [P, BLOCKS, D])
        acc = sb("acc", [P, BLOCKS * ROW])
        big = sb("big", [P, 2 * NPAD])
        hT = big[:, 0:NPAD]
        msg = big[:, NPAD:2 * NPAD]
        H = sb("H", [P, BLOCKS, D])
        dst_rel = sb("dst_rel", [P, KW])
        src_idx = sb("src_idx", [P, KW], I32)
        w_step = sb("w_step", [P, KW])
        type_step = sb("type_step", [P, KW])
        ring = sb("ring", [P, RING, ROW])
        onehot = sb("onehot", [P, RING, P])
        idx_stage = sb("idx_stage", [P, RING], I32)
        iota_k = sb("iota_k", [P, KW])
        pidx = sb("pidx", [P, 1])
        minus_p = sb("minus_p", [P, 1])
        kcol = sb("kcol", [P, KT])

        ident = sb("ident", [P, P])
        tri = sb("tri", [P, P])
        ones = sb("ones", [P, P])
        pad_i = sb("pad_i", [1, TAIL], I32)
        pad_z = sb("pad_z", [1, TAIL], I32)
        pad_f = sb("pad_f", [1, TAIL], F32)
        first_dst = sb("first_dst", [P, CT], I32)
        prev_dst = sb("prev_dst", [P, CT], I32)
        fb_i = sb("fb_i", [P, CT], I32)
        pb_i = sb("pb_i", [P, CT], I32)
        fb = sb("fb", [P, CT])
        pb = sb("pb", [P, CT])
        adv = sb("adv", [P, CT])
        adv_sum = sb("adv_sum", [P, CT])
        one13 = sb("one13", [P, BLOCKS])
        start_step = sb("start_step", [P, CT])
        pad_start = sb("pad_start", [P, 1])
        vw = sb("vw", [P, CT, 2], BF16)
        chunk_idx = sb("chunk_idx", [P, KT], I32)
        blk = sb("blk", [P, KT])
        neg_base = sb("neg_base", [P, KT])
        brow = sb("brow", [1, KW])
        off_row = sb("off_row", [1, KW], I32)
        stats = sb("stats", [P, BLOCKS, 6])
        mv = sb("mv", [P, BLOCKS, 2])
        ve = sb("ve", [P, BLOCKS])
        sd = sb("sd", [P, BLOCKS])
        rstd = sb("rstd", [P, BLOCKS])
        nmr = sb("nmr", [P, BLOCKS])
        types_at = sb("types_at", [P, BLOCKS, TYPES])
        typesT = H[0:TYPES, :, :].rearrange("p b f -> p (b f)")
        vw_before = types_at[:, :, :].rearrange("p b t -> p (b t)")[:, 0:CT].bitcast(BF16).rearrange("p (t a) -> p t a", a=2)
        degree = sb("degree", [P, BLOCKS])
        rcount = sb("rcount", [P, BLOCKS])
        dump = sb("dump", [P, 1])
        rows3 = sb("rows3", [3, RING, P], BF16)
        pick = sb("pick", [3, 2, P], BF16)
        equals = sb("equals", [P, RING])
        src_less = sb("src_less", [P, RING])
        last_src = sb("last_src", [P, RING])
        total = sb("total", [P, BLOCKS])
        before = sb("before", [P, BLOCKS])
        upto = sb("upto", [P, BLOCKS])
        empty = sb("empty", [P, BLOCKS])
        begin_i = sb("begin_i", [P, BLOCKS], I32)
        end_i = sb("end_i", [P, BLOCKS], I32)
        w_mean = sb("w_mean", [P, 2, D])
        b_mean = sb("b_mean", [P, D])
        w_raw = msg[:, 0:8 * D].rearrange("p (g f) -> p g f", g=8)
        wT = sb("wT", [P, 8, D])
        emb = sb("emb", [TYPES, D])
        emb_b = sb("emb_b", [TYPES, D])
        bcol = sb("bcol", [P, 6])
        brz = sb("brz", [P, 2])
        att_cols = sb("att_cols", [P, HA])
        w3 = sb("w3", [P, ROW3])
        gate = acc[:, 0:8 * QW].rearrange("p (a g w) -> p a g w", a=2, g=4)
        stage3 = onehot[:, :, :].rearrange("p a b -> p (a b)")[:, KW:KW + RING * HA].rearrange("p (u h) -> p u h", u=RING)
        first3 = first_dst[:, 0:1]
        first_logits = sb("first_logits", [P, HA])
        row_ends = type_step[:, 8 * P + 2 * BLOCKS * HEADS:8 * P + (2 * BLOCKS + 4) * HEADS]
        rowT = type_step[0:HEADS, 0:8 * P].rearrange("h (a p) -> h a p", a=8)
        carry = type_step[:, 8 * P + (2 * BLOCKS + 4) * HEADS:8 * P + (2 * BLOCKS + 6) * HEADS]
        sumsN = type_step[:, 8 * P:8 * P + BLOCKS * HEADS].rearrange("p (b h) -> p b h", h=HEADS)
        ratio = type_step[:, 8 * P + BLOCKS * HEADS:8 * P + 2 * BLOCKS * HEADS].rearrange("p (b h) -> p b h", h=HEADS)
        PS = ctx.enter_context(nc.psum_tensor("PS", [P, 8, 512], F32))

        consts_set = sem("consts_set")
        copied = sem("copied")
        x_loaded = sem("x_loaded")
        ends_loaded = sem("ends_loaded")
        w_loaded = sem("w_loaded")
        dve_done = sem("dve_done")
        att_folded = sem("att_folded")
        adv_ready = sem("adv_ready")
        adv_summed = sem("adv_summed")
        steps_marked = sem("steps_marked")
        steps_summed = sem("steps_summed")
        chunks_known = sem("chunks_known")
        rows_gathered = [sem(f"rows_gathered{n}") for n in range(4)]
        rows_ready = [sem(f"rows_ready{n}") for n in range(3)]
        rows_turned = sem("rows_turned")
        rows_stored = sem("rows_stored")
        zeros_ready = sem("zeros_ready")
        logits_zeroed = sem("logits_zeroed")
        ln_var = sem("ln_var")
        ln_sd = sem("ln_sd")
        ln_scale = sem("ln_scale")
        ln_relu = sem("ln_relu")
        table_written = sem("table_written")
        h_turned = sem("h_turned")
        h_stored = sem("h_stored")
        staged = sem("staged")
        pool_passed = sem("pool_passed")
        gathered = [sem(f"gathered{u}") for u in range(RING)]
        parts_made = sem("parts_made")
        rows_parted = sem("rows_parted")
        backs_zeroed = sem("backs_zeroed")
        rows3_loaded = [sem(f"rows3_loaded{q}") for q in range(RING // Q)]
        spread = sem("spread")
        same_raw = sem("same_raw")
        picks_ready = sem("picks_ready")
        same_ready = sem("same_ready")
        equals_ready = sem("equals_ready")
        less_ready = sem("less_ready")
        void_marked = sem("void_marked")
        places_ready = sem("places_ready")
        rows_picked = sem("rows_picked")
        rows_weighted = sem("rows_weighted")
        equals_summed = sem("equals_summed")
        sums_taken = sem("sums_taken")
        scattered = [sem(f"scattered{n}") for n in range(COPIES)]
        pieces_loaded = [sem(f"pieces_loaded{n}") for n in range(2)]
        piece_added = sem("piece_added")
        mean_ready = sem("mean_ready")
        mean_turned = sem("mean_turned")
        mean_stored = sem("mean_stored")
        hot_ready = sem("hot_ready")
        summed = sem("summed")
        added = sem("added")
        degree_ready = sem("degree_ready")
        nodes_summed = sem("nodes_summed")
        nodes_counted = sem("nodes_counted")
        types_turned = sem("types_turned")
        types_stored = sem("types_stored")
        w_turned = sem("w_turned")
        wT_ready = sem("wT_ready")
        mean_summed = sem("mean_summed")
        mean_added = sem("mean_added")
        msg_summed = sem("msg_summed")
        msg_stored = sem("msg_stored")
        gates_summed = sem("gates_summed")
        rz_ready = sem("rz_ready")
        n_summed = sem("n_summed")
        n_ready = sem("n_ready")
        gru_ready = sem("gru_ready")
        gru_turned = sem("gru_turned")
        gru_added = sem("gru_added")
        att_summed = sem("att_summed")
        att_stored = sem("att_stored")
        w3_ready = sem("w3_ready")
        logits_written = sem("logits_written")
        starts_written = sem("starts_written")
        last_loaded = sem("last_loaded")
        first_back = sem("first_back")
        filled_back = sem("filled_back")
        staged3 = sem("staged3")
        gathered3 = [sem(f"gathered3_{q}") for q in range(4)]
        ring_cleared = sem("ring_cleared")
        src3_loaded = sem("src3_loaded")
        low_made = sem("low_made")
        low_turned = sem("low_turned")
        low_ready = sem("low_ready")
        low_stored = sem("low_stored")
        lows_loaded = [sem(f"lows_loaded{n}") for n in range(2)]
        parts3_ready = sem("parts3_ready")
        low_spread = sem("low_spread")
        low_apart = sem("low_apart")
        low_hot = [sem(f"low_hot{v}") for v in range(2)]
        high_hot = sem("high_hot")
        picked3 = sem("picked3")
        multiplied3 = sem("multiplied3")
        picked_logits = sem("picked_logits")
        all_logits = sem("all_logits")
        ends_turn = sem("ends_turn")
        turned3 = sem("turned3")
        carry_row = sem("carry_row")
        exp_in = sem("exp_in")
        exp_out = sem("exp_out")
        sums_ready = sem("sums_ready")
        sums_written = sem("sums_written")
        sums_back = [sem(f"sums_back{n}") for n in range(FINAL)]
        bias_added = sem("bias_added")
        counts_ready = sem("counts_ready")
        places_scaled = sem("places_scaled")
        out_ready = sem("out_ready")
        out_written = sem("out_written")

        HWv = acc[:, 0:BLOCKS * ROW3].rearrange("p (b r) -> p b r", r=ROW3)
        al = hT[:, 0:CHUNKS * HEADS]
        al3 = al.rearrange("p (j h) -> p j h", h=HEADS)
        aj = H[:, :, :].rearrange("p b f -> p (b f)")[:, 0:CHUNKS * HEADS]
        aj3 = aj.rearrange("p (j h) -> p j h", h=HEADS)
        mx = msg[:, 0:CHUNKS * HEADS]
        mx3 = mx.rearrange("p (j h) -> p j h", h=HEADS)
        flat_ring = ring[:, :, :].rearrange("p a b -> p (a b)")
        flat_hot = onehot[:, :, :].rearrange("p a b -> p (a b)")
        dst3 = flat_ring[:, 0:CHUNKS].bitcast(I32)
        prev3 = flat_hot[:, 0:CHUNKS].bitcast(I32)
        not_start = w_step[:, 0:CHUNKS]
        start_low = dst_rel[:, 0:CHUNKS]
        src3 = src_idx[:, 0:CHUNKS]
        AN = CHUNKS * HEADS
        raw3 = flat_ring[:, 0:KW].bitcast(I32)
        low_i = flat_hot[:, 0:KW].bitcast(I32)
        lowT = flat_hot[:, 0:KW // 2].bitcast(BF16)
        B3 = 2 * G3
        taken = [0]

        def part_of_msg(columns):
            taken[0] += columns
            return msg[:, taken[0] - columns:taken[0]]

        products = part_of_msg(2 * B3 * HM).rearrange("p (n s m) -> p n s m", n=2, m=HM)
        highs = part_of_msg(2 * B3 * HIGHS).rearrange("p (n s b) -> p n s b", n=2, b=HIGHS)
        apart = part_of_msg(2 * G3 * P).bitcast(BF16).rearrange("p (n k) -> p n k", n=4)
        low_hots = [part_of_msg(2 * G3 * P).bitcast(BF16).rearrange("p (n k) -> p n k", n=4) for v in range(2)]
        lows = type_step[0:1, 0:B3 * P].bitcast(BF16).rearrange("p (n s e) -> p n s e", n=2, e=P)
        parts3 = part_of_msg(3 * HM).bitcast(BF16).rearrange("p (a v m) -> p a v m", a=3, v=2)
        left3 = products[:, 0, 0:2, :]
        spread_bank = (0, 1, 6, 7)
        ones_row = flat_ring[0:1, KW:KW + P // 2].bitcast(BF16)

        dstT = onehot[:, 0:2 * Q, :]
        same = onehot[:, 2 * Q:4 * Q, :]
        picked = flat_ring[:, 0:2 * Q * MROW].rearrange("p (s r) -> p s r", r=MROW)
        sums_out = flat_ring[:, 2 * Q * MROW:(2 * Q + COPIES) * MROW].rearrange("p (s r) -> p s r", r=MROW)
        in_block = type_step
        acc_m = acc[:, 0:BLOCKS * MROW].rearrange("p (b r) -> p b r", r=MROW)
        pieces = [msg[:, n * COPIES * PIECE * MROW:(n + 1) * COPIES * PIECE * MROW] for n in range(2)]
        meanT = onehot[:, :, :].rearrange("p a b -> p (a b)")[:, 0:2 * LNG * P].rearrange("p (n k) -> p n k", n=2)
        rows3_bf = hT[:, 0:3 * KW // 2].bitcast(BF16).rearrange("p (a k) -> p a k", a=3)
        src_high = hT[:, 3 * KW // 2:5 * KW // 2].bitcast(I32)
        src_low = hT[:, 5 * KW // 2:7 * KW // 2].bitcast(I32)

        marks = big[:, 0:CT * P].bitcast(BF16).rearrange("p (t k) -> p t k", k=2 * P)
        ones_bf = big[:, CT * P:CT * P + P // 2].bitcast(BF16)
        rows = [acc[:, n * KW:(n + 1) * KW] for n in range(3)] + [hT[:, 0:KW]]
        rows_i = [r.bitcast(I32) for r in rows]
        acc_d = acc[:, 0:NPAD]
        h_flat = H[:, :, :].rearrange("p b f -> p (b f)")

        def slot(u, w):
            return PS[:, u // 2, (u % 2) * 256:(u % 2) * 256 + w]

        block = ctx.enter_context(nc.Block())

        @block.sync
        def _(sp):
            sp.wait_ge(ring_cleared, 1)
            sp.dma_start(raw3[0:P - 1, 0:CHUNKS], src[0:(P - 1) * CHUNKS].rearrange("(p j) -> p j", p=P - 1)
                         ).then_inc(src3_loaded, 16)
            sp.dma_start(raw3[P - 1:P, 0:CHUNKS - TAIL], src[(P - 1) * CHUNKS:EDGES].rearrange("(p j) -> p j", p=1)
                         ).then_inc(src3_loaded, 16)
            sp.wait_ge(consts_set, 1)
            sp.wait_ge(ends_loaded, 128)
            for full, pad, tail in ((dst_pad, dst, pad_i), (src_pad, src, pad_z), (type_pad, edge_type, pad_z),
                                    (weight_pad, edge_weight, pad_f)):
                sp.dma_start(full[0:EDGES].rearrange("(a b) -> a b", a=16), pad.rearrange("(a b) -> a b", a=16)
                             ).then_inc(copied, 16)
                sp.dma_start(full[EDGES:EPAD].rearrange("(a b) -> a b", a=1), tail[:, :]).then_inc(copied, 16)
            whole = (BLOCKS - 1) * P
            sp.dma_start(X[:, 0:BLOCKS - 1, :], x[0:whole, :].rearrange("(b p) f -> p b f", p=P)).then_inc(x_loaded, 16)
            sp.dma_start(X[0:LAST, BLOCKS - 1, :], x[whole:NODES, :]).then_inc(x_loaded, 16)
            sp.dma_start(w_mean[:, :, :], mean_w.rearrange("(a f) o -> f a o", a=2)).then_inc(w_loaded, 16)
            sp.dma_start(b_mean[:, :], mean_b.rearrange("(a o) -> a o", a=1).broadcast_to([P, D])
                         ).then_inc(w_loaded, 16)
            sp.dma_start(w3[:, 0:D], att_w).then_inc(w_loaded, 16)
            sp.dma_start(emb[:, :], embed).then_inc(w_loaded, 16)
            sp.dma_start(emb_b[:, :], msg_b.rearrange("(a o) -> a o", a=1).broadcast_to([TYPES, D])).then_inc(w_loaded, 16)
            with nc.allow_non_contiguous_dma("a few columns of biases"):
                sp.dma_start(bcol[:, 0:3], b_ih.rearrange("(g j) -> j g", g=3)).then_inc(w_loaded, 16)
                sp.dma_start(bcol[:, 3:6], b_hh.rearrange("(g j) -> j g", g=3)).then_inc(w_loaded, 16)
                for h in range(HEADS):
                    sp.dma_start(att_cols[h * C:(h + 1) * C, h:h + 1], att[0, h:h + 1, 0:C].rearrange("a c -> c a")
                                 ).then_inc(w_loaded, 16)
                    sp.dma_start(att_cols[h * C:(h + 1) * C, HEADS + h:HEADS + h + 1],
                                 att[0, h:h + 1, C:2 * C].rearrange("a c -> c a")).then_inc(w_loaded, 16)
            def write_table(n, norm, groups):
                for g in groups:
                    sp.wait_ge(ln_relu, NLN * norm + g + 1)
                    b0, b1 = g * LNG, min(BLOCKS, (g + 1) * LNG)
                    sp.dma_start(tables[n][b0 * P:b1 * P, :].rearrange("(b p) f -> p b f", p=P),
                                 H[:, b0:b1, :]).then_inc(table_written, 16)

            sp.wait_ge(low_ready, 1)
            sp.dma_start(low_rows.rearrange("(t p) e -> p t e", p=P), lowT.rearrange("p (t e) -> p t e", e=P)
                         ).then_inc(low_stored, 16)
            write_table(0, 0, range(NLN))
            sp.wait_ge(parts_made, 1)
            for a in range(3):
                sp.dma_start(edge_rows[:, a, :].rearrange("(t p) e -> p t e", p=P),
                             rows3_bf[:, a, :].rearrange("p (t e) -> p t e", e=P)).then_inc(rows_parted, 16)
            sp.wait_ge(zeros_ready, 1)
            for n in range(COPIES):
                half = (NPAD + P) // 2 * MROW
                for v in range(2):
                    sp.wait_ge(summed, (2 * n + v + 1) * (STEPS // (2 * COPIES + 3)))
                    sp.dma_start(back[n].rearrange("k r -> (k r)")[v * half:(v + 1) * half].rearrange("(p m) -> p m", p=P),
                                 msg[:, 0:half // P]).then_inc(backs_zeroed, 16)
            sp.dma_start(start_logits.rearrange("(p j) h -> p (j h)", p=P), mx).then_inc(logits_zeroed, 16)
            sp.wait_ge(logits_zeroed, 16)
            sp.wait_ge(backs_zeroed, 32 * COPIES)
            sp.dma_start(w_raw[:, 0, :], msg_w).then_inc(w_loaded, 16)
            sp.dma_start(w_raw[:, 1:4, :], w_ih.rearrange("(g j) f -> j g f", g=3)).then_inc(w_loaded, 16)
            sp.dma_start(w_raw[:, 4:7, :], w_hh.rearrange("(g j) f -> j g f", g=3)).then_inc(w_loaded, 16)
            sp.dma_start(w_raw[:, 7, :], att_w).then_inc(w_loaded, 16)
            sp.wait_ge(rows_parted, 48)

            def load_rows3(i, q):
                sp.dma_start(rows3[:, q * Q:(q + 1) * Q, :],
                             edge_rows[bass.ds(i * RING + q * Q, Q), :, :].rearrange("k a e -> a k e")
                             ).then_inc(rows3_loaded[q], 16)

            for q in range(RING // Q):
                load_rows3(0, q)
            with sp.Fori(0, ITERS - 1) as i:
                for q in range(RING // Q):
                    sp.wait_ge(spread, i * (RING // Q) + (q + 1))
                    load_rows3(i + 1, q)
            for n in range(COPIES):
                sp.wait_ge(scattered[n], 32 * ITERS)
            AHEAD = 6
            for c in range(PIECES):
                b0, nb = c * PIECE, min(PIECE, BLOCKS - c * PIECE)
                if c >= 2:
                    sp.wait_ge(piece_added, c - 1)
                to = pieces[c % 2][:, 0:COPIES * nb * MROW].rearrange("p (n b r) -> p n b r", n=COPIES, r=MROW)
                for n in range(COPIES):
                    sp.dma_start(to[:, n, :, :], back[n][b0 * P:(b0 + nb) * P, :].rearrange("(b p) r -> p b r", p=P)
                                 ).then_inc(pieces_loaded[c % 2], 16)
                if c >= AHEAD and c % 2 == 0:
                    write_table(1, 2, [(c - AHEAD) // 2])
            write_table(1, 2, range((PIECES - 1 - AHEAD) // 2 + 1, NLN))
            sp.wait_ge(added, 2 * STEPS)
            sp.wait_ge(summed, 2 * STEPS)
            sp.wait_ge(staged, 2 * ITERS * 2)
            sp.dma_start(dst3, dst_pad.rearrange("(p j) -> p j", p=P)).then_inc(last_loaded, 16)
            sp.dma_start(prev3[1:P, :], dst_pad[CHUNKS - 1:EPAD - 1].rearrange("(p j) -> p j", p=P - 1)
                         ).then_inc(last_loaded, 16)
            sp.dma_start(prev3[0:1, 1:CHUNKS], dst_pad[0:CHUNKS - 1].rearrange("(p j) -> p j", p=1)
                         ).then_inc(last_loaded, 16)
            with nc.allow_non_contiguous_dma("the first destination of each row"):
                sp.dma_start(first3[:, :], dst_pad.rearrange("(p j) -> p j", p=P)[:, 0:1]).then_inc(last_loaded, 16)
            sp.dma_start(src3[:, 0:CHUNKS], src_pad.rearrange("(p j) -> p j", p=P)).then_inc(last_loaded, 16)
            sp.wait_ge(att_stored, NATT)
            sp.dma_start(logit_table.rearrange("(b p) h -> p b h", p=P), HWv[:, :, D:ROW3]).then_inc(logits_written, 16)

            def load_lows(i, m):
                sp.dma_start(lows[:, m % 2, :, :], low_rows[bass.ds(i * COLS3 + m * 2 * G3, 2 * G3), :].unsqueeze(0)
                             ).then_inc(lows_loaded[m % 2], 16)

            def low_round(i, first):
                for m in range(first, COLS3 // (2 * G3)):
                    sp.wait_ge(low_spread, i * GROUPS3 + 2 * (m - 1))
                    load_lows(i, m)

            for m in range(2):
                load_lows(0, m)
            low_round(0, 2)
            with sp.Fori(1, IT3 // 2 - 2) as i:
                low_round(i, 0)
            sp.wait_ge(starts_written, 16 * BLOCKS)
            sp.dma_start(aj, start_logits.rearrange("(p j) h -> p (j h)", p=P)).then_inc(filled_back, 16)
            with sp.Fori(IT3 // 2 - 2, IT3) as i:
                low_round(i, 0)
            sp.wait_ge(sums_ready, 1)
            sp.dma_start(sums_dram.rearrange("(p j) h -> p (j h)", p=P), mx).then_inc(sums_written, 16)
            for n in range(FINAL):
                sp.wait_ge(out_ready, n + 1)
                b0, b1 = n * FB, min(BLOCKS - 1, (n + 1) * FB)
                sp.dma_start(out[b0 * P:b1 * P, :].rearrange("(b p) f -> p b f", p=P), X[:, b0:b1, :]).then_inc(out_written, 16)
            sp.dma_start(out[whole:NODES, :], X[0:LAST, BLOCKS - 1, :]).then_inc(out_written, 16)
            sp.wait_ge(out_written, 16 * (FINAL + 1))

        @block.gpsimd
        def _(pool):
            pool.memset(pad_i[:, :], NOBODY)
            pool.memset(pad_z[:, :], 0)
            pool.memset(att_cols[:, :], 0.0)
            pool.memset(X[:, BLOCKS - 1, :], 0.0)
            pool.memset(pad_f[:, :], 0.0).then_inc(consts_set, 1)
            pool.iota(iota_k[:, :], pattern=[[1, KW]], base=0, channel_multiplier=0,
                      allow_small_or_imprecise_dtypes=True)
            pool.iota(pidx[:, :], pattern=[[0, 1]], base=0, channel_multiplier=1, allow_small_or_imprecise_dtypes=True)
            pool.iota(kcol[:, :], pattern=[[P, KT]], base=0, channel_multiplier=1,
                      allow_small_or_imprecise_dtypes=True).then_inc(consts_set, 1)
            pool.memset(first_dst[:, :], 0)
            pool.memset(prev_dst[:, :], -P).then_inc(consts_set, 1)
            pool.wait_ge(consts_set, 3)
            with nc.allow_non_contiguous_dma("one number of each chunk"):
                for full, at, off in ((first_dst, 0, 0), (prev_dst, 1, P - 1)):
                    body, tail = P * P, (CT - 1) * P * P
                    pool.dma_start(full[at:P, 0:1], dst[off:off + (P - at) * P].rearrange("(p e) -> p e", e=P)[:, 0:1]
                                   ).then_inc(ends_loaded, 16)
                    lead = off - at * P
                    pool.dma_start(full[:, 1:CT - 1], dst[body + lead:tail + lead].rearrange("(t p e) -> p t e", p=P, e=P)[:, :, 0]
                                   ).then_inc(ends_loaded, 16)
                    pool.dma_start(full[0:CREST - 1, CT - 1:CT],
                                   dst[tail + lead:tail + lead + (CREST - 1) * P].rearrange("(p e) -> p e", e=P)[:, 0:1]
                                   ).then_inc(ends_loaded, 16)
                    z = tail + lead + (CREST - 1) * P
                    pool.dma_start(full[CREST - 1:CREST, CT - 1:CT], dst[z:z + 1].rearrange("(p e) -> p e", p=1)
                                   ).then_inc(ends_loaded, 16)
            pool.wait_ge(copied, 128)
            pool.wait_ge(chunks_known, 1)

            def gather_rows(n, pad):
                view = pad.rearrange("(c e) -> c e", e=P)
                dest = rows[n] if n == 3 else rows_i[n]
                for t in range(KT):
                    pool.indirect_dma_start(dest[:, t * P:(t + 1) * P], None, view,
                                            bass.IndirectOffsetOnAxis(ap=chunk_idx[:, t:t + 1], axis=0)
                                            ).then_inc(rows_gathered[n], 16)

            for n, pad in enumerate((dst_pad, src_pad, type_pad)):
                gather_rows(n, pad)

            def edge_gathers(turn):
                pool.wait_ge(table_written, 16 * NLN * (turn + 1))
                with pool.Fori(0, ITERS) as i:
                    for h in range(2):
                        pool.wait_ge(staged, i * 2 + (2 * ITERS * turn + h + 1))
                        pool.sem_inc(pool_passed, 1)
                        for u in range(h * HALF, (h + 1) * HALF):
                            pool.indirect_dma_start(ring[:, u, 0:D], None, tables[turn],
                                                    bass.IndirectOffsetOnAxis(ap=idx_stage[:, u:u + 1], axis=0)
                                                    ).then_inc(gathered[u], 16)

            edge_gathers(0)

            pool.wait_ge(rows_parted, 48)
            gather_rows(3, weight_pad)
            pool.wait_ge(backs_zeroed, 32 * COPIES)

            def scatter(q):
                for s in range(Q):
                    u = q * Q + s
                    pool.indirect_dma_start(back[u % COPIES], bass.IndirectOffsetOnAxis(ap=idx_stage[:, u:u + 1], axis=0),
                                            sums_out[:, u % COPIES, :], None, compute_op=ALU.add
                                            ).then_inc(scattered[u % COPIES], 16)

            with pool.Fori(0, ITERS) as i:
                for q in range(RING // Q):
                    pool.wait_ge(sums_taken, i * (RING // Q) + (q + 1))
                    pool.sem_inc(pool_passed, 1)
                    scatter(q)

            edge_gathers(1)

            pool.wait_ge(logits_zeroed, 16)
            pool.wait_ge(att_stored, NATT)
            pool.wait_ge(nodes_counted, 1)
            for b in range(BLOCKS):
                pool.indirect_dma_start(start_logits, bass.IndirectOffsetOnAxis(ap=begin_i[:, b:b + 1], axis=0),
                                        HWv[:, b, D + HEADS:ROW3], None, bounds_check=EPAD - 1, oob_is_err=False
                                        ).then_inc(starts_written, 16)
            pool.wait_ge(logits_written, 16)
            pool.wait_ge(last_loaded, 80)
            pool.indirect_dma_start(first_logits[:, :], None, logit_table,
                                    bass.IndirectOffsetOnAxis(ap=first3[:, 0:1], axis=0)).then_inc(first_back, 16)

            def gather_round(i, columns):
                for q in range(ceil_div(columns, QUARTER)):
                    pool.wait_ge(staged3, i * 4 + (q + 1))
                    pool.sem_inc(pool_passed, 1)
                    for u in range(q * QUARTER, min(columns, (q + 1) * QUARTER)):
                        pool.indirect_dma_start(stage3[:, u, :], None, logit_table,
                                                bass.IndirectOffsetOnAxis(ap=idx_stage[:, u:u + 1], axis=0)
                                                ).then_inc(gathered3[q], 16)

            with pool.Fori(0, ROUNDS3 - 1) as i:
                gather_round(i, RING3)
            gather_round(ROUNDS3 - 1, TAIL3)
            pool.wait_ge(sums_written, 16)
            for b in range(BLOCKS):
                pool.indirect_dma_start(sumsN[:, b, :], None, sums_dram,
                                        bass.IndirectOffsetOnAxis(ap=end_i[:, b:b + 1], axis=0),
                                        bounds_check=EPAD - 1, oob_is_err=False).then_inc(sums_back[b // FB], 16)

        @block.scalar
        def _(act):
            def deviations(n, g):
                b0, b1 = g * LNG, min(BLOCKS, (g + 1) * LNG)
                act.wait_ge(ln_var, NLN * n + g + 1)
                act.activation(sd[:, b0:b1], ve[:, b0:b1], ACT.Sqrt).then_inc(ln_sd, 1)

            def normalize(n, g):
                act.wait_ge(ln_scale, NLN * n + g + 1)
                if g == 0 and n in (1, 3):
                    act.wait_ge(table_written, 16 * NLN * (1 if n == 1 else 2))
                for b in range(g * LNG, min(BLOCKS, (g + 1) * LNG)):
                    ins = act.activation(H[:, b, :], X[:, b, :], ACT.Relu, bias=nmr[:, b:b + 1], scale=rstd[:, b:b + 1])
                ins.then_inc(ln_relu, 1)

            def layer_norm(n):
                deviations(n, 0)
                for g in range(NLN):
                    if g < NLN - 1:
                        deviations(n, g + 1)
                    normalize(n, g)

            def store_h(n):
                for q in range(ceil_div(BLOCKS, 4)):
                    w = min(4, BLOCKS - 4 * q) * P
                    act.wait_ge(h_turned, ceil_div(BLOCKS, 4) * (n - 1) + q + 1)
                    act.activation(hT[:, q * 512:q * 512 + w], PS[:, q % 8, 0:w], ACT.Copy).then_inc(h_stored, 1)

            def edge_stages(turn):
                def stage(i, h):
                    act.activation(idx_stage[:, h * HALF:(h + 1) * HALF], src_idx[:, bass.ds(i * RING + h * HALF, HALF)],
                                   ACT.Copy).then_inc(staged, 1)

                for h in range(2):
                    stage(0, h)
                with act.Fori(0, ITERS - 1) as i:
                    for h in range(2):
                        act.wait_ge(summed, i * RING + (STEPS * turn + (h + 1) * HALF))
                        stage(i + 1, h)

            act.wait_ge(low_turned, 1)
            act.activation(lowT, PS[:, 4:8, :].rearrange("p a b -> p (a b)")[:, 0:KW], ACT.Copy).then_inc(low_ready, 1)
            layer_norm(0)
            act.wait_ge(parts_made, 1)
            act.activation(rows[1], rows_i[1], ACT.Copy).then_inc(rows_ready[1], 1)

            def turned_out(n, dest, want):
                act.wait_ge(rows_turned, want)
                base = 4 * (n % 2)
                flat = PS[:, base:base + 4, :].rearrange("p a b -> p (a b)")
                act.activation(dest[:, 0:KW], flat[:, 0:KW], ACT.Copy).then_inc(rows_stored, 1)

            turned_out(0, dst_rel, 1)
            turned_out(1, src_idx, 2)
            turned_out(2, type_step, 3)
            act.wait_ge(rows_stored, 3)
            edge_stages(0)
            for q in range(2):
                act.wait_ge(w_turned, q + 1)
                act.activation(wT[:, 4 * q:4 * q + 4, :].rearrange("p a b -> p (a b)"), PS[:, 2 + q, :], ACT.Copy
                               ).then_inc(wT_ready, 1)
            layer_norm(1)
            turned_out(3, w_step, 4)
            act.wait_ge(rows_stored, 4)

            GI = RING // Q

            def weigh(i, q):
                act.wait_ge(rows_picked, i * GI + (q + 1))
                for s in range(Q):
                    act.activation(picked[:, (q % 2) * Q + s, 0:D], PS[:, 2 + q % 2, s * P:(s + 1) * P], ACT.Copy,
                                   scale=w_step[:, bass.ds(i * RING + (q * Q + s), 1)])
                act.activation(picked[:, (q % 2) * Q:(q % 2 + 1) * Q, D], in_block[:, bass.ds(i * RING + q * Q, Q)], ACT.Copy
                               ).then_inc(rows_weighted, 1)

            def take(i, q):
                act.wait_ge(equals_summed, i * GI + (q + 1))
                act.wait_ge(places_ready, i * GI + (q + 1))
                for s in range(0, Q, 2):
                    u = q * Q + s
                    for v in (u, u + 1):
                        if not (isinstance(i, int) and i == 0 and v < COPIES):
                            act.wait_ge(scattered[v % COPIES], i * 32 + 16 * (v // COPIES))
                    bank = 4 + 2 * (q % 2) + s // 2
                    ins = act.activation(sums_out[:, u % COPIES:u % COPIES + 2, :],
                                         PS[:, bank, :].rearrange("p (s r) -> p s r", s=2)[:, :, 0:MROW], ACT.Copy)
                ins.then_inc(sums_taken, 1)

            def back_round(i, first):
                for q in range(GI):
                    weigh(i, q)
                    if q or not first:
                        take(i if q else i - 1, (q - 1) % GI)

            back_round(0, True)
            with act.Fori(1, ITERS) as i:
                back_round(i, False)
            take(ITERS - 1, GI - 1)
            store_h(1)
            for g in range(NLN):
                b0, b1 = g * LNG, min(BLOCKS, (g + 1) * LNG)
                act.wait_ge(counts_ready, g + 1)
                for b in range(b0, b1):
                    ins = act.activation(acc_m[:, b, 0:D], acc_m[:, b, 0:D], ACT.Copy, scale=rcount[:, b:b + 1])
                ins.then_inc(mean_ready, 1)
                w = (b1 - b0) * P
                act.wait_ge(mean_turned, g + 1)
                act.activation(meanT[:, g % 2, 0:w], PS[:, 2 * (g % 2):2 * (g % 2) + 2, :].rearrange("p a b -> p (a b)")[:, 0:w],
                               ACT.Copy).then_inc(mean_stored, 1)
                if g:
                    deviations(2, g - 1)
                    normalize(2, g - 1)
            deviations(2, NLN - 1)
            normalize(2, NLN - 1)
            store_h(2)
            edge_stages(1)
            act.wait_ge(table_written, 16 * NLN * 2)
            for q in range(ceil_div(BLOCKS, 4)):
                w = min(4, BLOCKS - 4 * q) * P
                act.wait_ge(types_turned, q + 1)
                act.activation(typesT[:, q * 512:q * 512 + w], PS[0:TYPES, q % 8, 0:w], ACT.Copy).then_inc(types_stored, 1)
            for q in range(ceil_div(NPAD, 512)):
                w = min(512, NPAD - 512 * q)
                act.wait_ge(msg_summed, q + 1)
                act.activation(msg[:, q * 512:q * 512 + w], PS[:, q % 2, 0:w], ACT.Copy).then_inc(msg_stored, 1)
            for q in range(NQ):
                w = min(QW, NPAD - QW * q)
                act.wait_ge(gates_summed, q + 1)
                if q >= 2:
                    act.wait_ge(gru_turned, q - 1)
                pr = 2 + 2 * (q % 2)
                act.activation(gate[:, q % 2, 0, 0:w], PS[:, pr, 0:w], ACT.Sigmoid, bias=brz[:, 0:1]).then_inc(rz_ready, 1)
                act.activation(gate[:, q % 2, 1, 0:w], PS[:, pr, QW:QW + w], ACT.Sigmoid, bias=brz[:, 1:2]).then_inc(rz_ready, 1)
                act.wait_ge(n_summed, q + 1)
                act.activation(gate[:, q % 2, 2, 0:w], gate[:, q % 2, 3, 0:w], ACT.Tanh, bias=bcol[:, 2:3]).then_inc(n_ready, 1)
            layer_norm(3)
            store_h(3)
            for q in range(ceil_div(BLOCKS, 3)):
                k = min(3, BLOCKS - 3 * q)
                act.wait_ge(att_summed, q + 1)
                ins = act.activation(HWv[:, 3 * q:3 * q + k, :].rearrange("p b r -> p (b r)"), PS[:, q % 8, 0:k * ROW3], ACT.Copy)
                ins.then_inc(att_stored, 1)

            act.wait_ge(last_loaded, 80)

            def quarter(i, q):
                if isinstance(i, int) and i >= ROUNDS3 - 1:
                    return min(QUARTER, max(0, TAIL3 - q * QUARTER)) if i == ROUNDS3 - 1 else 0
                return QUARTER

            def stage3_in(i, q):
                k = quarter(i, q)
                if k:
                    act.activation(idx_stage[:, q * QUARTER:q * QUARTER + k],
                                   src3[:, bass.ds(i * RING3 + (ONEHOT_COLS + q * QUARTER), k)], ACT.Copy).then_inc(staged3, 1)

            def stage3_out(i, q):
                k = quarter(i, q)
                if k:
                    act.wait_ge(gathered3[q], i * (16 * QUARTER) + 16 * k)
                    act.activation(al3[:, bass.ds(i * RING3 + (ONEHOT_COLS + q * QUARTER), k), :],
                                   stage3[:, q * QUARTER:q * QUARTER + k, 0:HEADS], ACT.Copy).then_inc(all_logits, 1)

            def low_hots3(i, g):
                n = i * GROUPS3 + g
                act.wait_ge(low_spread, n + 1)
                if not (isinstance(i, int) and i == 0 and g < 4):
                    act.wait_ge(low_hot[1], n - 3)
                act.activation(apart[:, g % 4, :], PS[:, spread_bank[g % 4], :], ACT.Abs, bias=minus_p[:, 0:1]
                               ).then_inc(low_apart, 1)
                act.wait_ge(low_apart, n + 1)
                if not (isinstance(i, int) and i == 0 and g < 4):
                    act.wait_ge(picked3, n - 3)
                act.activation(low_hots[0][:, g % 4, :], apart[:, g % 4, :], ACT.Relu, bias=1.0, scale=-1.0
                               ).then_inc(low_hot[0], 1)

            def logit_round(i, gathers):
                for q in range(4):
                    for g in range(q * GROUPS3 // 4, (q + 1) * GROUPS3 // 4):
                        low_hots3(i, g)
                    if gathers:
                        r = i - LATE3
                        stage3_out(r, q)
                        if quarter(r + 1 if isinstance(r, int) else r, q):
                            act.wait_ge(all_logits, r * 4 + (q + 1))
                            stage3_in(r + 1, q)

            for q in range(4):
                stage3_in(0, q)
            logit_round(0, False)
            with act.Fori(1, LATE3) as i:
                logit_round(i, False)
            with act.Fori(LATE3, LATE3 + ROUNDS3 - 2) as i:
                logit_round(i, True)
            for i in range(LATE3 + ROUNDS3 - 2, IT3):
                logit_round(i, i < LATE3 + ROUNDS3)
            act.wait_ge(exp_in, 1)
            act.activation(aj, aj, ACT.Exp).then_inc(exp_out, 1)
            act.wait_ge(exp_in, 2)
            act.activation(al[:, 0:AN], al[:, 0:AN], ACT.Exp).then_inc(exp_out, 1)
            act.wait_ge(exp_in, 3)
            act.activation(rowT[:, 5, :], rowT[:, 5, :], ACT.Exp).then_inc(exp_out, 1)

        @block.tensor
        def _(pe):
            pe.wait_ge(adv_ready, 1)
            pe.matmul(PS[:, 0, 0:CT], tri[:, :], adv[:, :], start=True, stop=False)
            pe.matmul(PS[:, 0, 0:CT], ones[:, :], adv_sum[:, :], start=False, stop=True).then_inc(adv_summed, 1)
            pe.wait_ge(low_made, 1)
            for t in range(KT):
                ins = pe.transpose(PS[:, 4 + t // 4, (t % 4) * P:(t % 4 + 1) * P], flat_ring[:, t * P:(t + 1) * P], ident[:, :])
            ins.then_inc(low_turned, 1)
            pe.wait_ge(steps_marked, 1)
            for k in range(KT):
                parts = [(ones_bf, vw_before[:, k - 1, :])] if k >= 2 else []
                parts += [(marks[:, t, (k - t) * P:(k - t + 1) * P], vw[:, t, :]) for t in range(max(0, k - 1), k + 1)]
                for n, (mark, value) in enumerate(parts):
                    pe.matmul(PS[:, 1, 2 * k:2 * k + 2], mark, value, start=(n == 0), stop=(n == len(parts) - 1))
            pe.wait_ge(low_ready, 1)
            for k in range(KT):
                parts = [(ones_bf, vw_before[:, k - 1, 1:2])] if k >= 2 else []
                parts += [(marks[:, t, (k - t) * P:(k - t + 1) * P], vw[:, t, 1:2]) for t in range(max(0, k - 1), k + 1)]
                for n, (mark, value) in enumerate(parts):
                    ins = pe.matmul(PS[0:1, 2 + k // 4, (k % 4) * P:(k % 4 + 1) * P], value, mark,
                                    start=(n == 0), stop=(n == len(parts) - 1))
            ins.then_inc(steps_summed, 1)
            pe.wait_ge(chunks_known, 2)

            def turn_rows(n):
                if n < 3:
                    pe.wait_ge(rows_ready[n], 1)
                else:
                    pe.wait_ge(rows_gathered[3], 16 * KT)
                if n >= 2:
                    pe.wait_ge(rows_stored, n - 1)
                for t in range(KT):
                    ins = pe.transpose(PS[:, 4 * (n % 2) + t // 4, (t % 4) * P:(t % 4 + 1) * P], rows[n][:, t * P:(t + 1) * P],
                                       ident[:, :])
                ins.then_inc(rows_turned, 1)

            for n in range(3):
                turn_rows(n)
            pe.wait_ge(rows_stored, 3)

            def turn_h(n):
                for q in range(ceil_div(BLOCKS, 4)):
                    if q >= 8:
                        pe.wait_ge(h_stored, ceil_div(BLOCKS, 4) * (n - 1) + q - 7)
                    k = min(4, BLOCKS - 4 * q)
                    pe.wait_ge(ln_relu, NLN * n + (4 * q + k - 1) // LNG + 1)
                    for j in range(k):
                        ins = pe.transpose(PS[:, q % 8, j * P:(j + 1) * P], H[:, 4 * q + j, :], ident[:, :])
                    ins.then_inc(h_turned, 1)
                pe.wait_ge(h_stored, ceil_div(BLOCKS, 4) * n)

            def edge_sums(turn):
                with pe.Fori(0, ITERS) as i:
                    for h in range(2):
                        pe.wait_ge(hot_ready, i * 2 + (2 * ITERS * turn + h + 1))
                        for u in range(h * HALF, (h + 1) * HALF):
                            pe.wait_ge(gathered[u], i * 16 + (16 * ITERS * turn + 16))
                            if turn == 0:
                                pe.matmul(slot(u, ROW), onehot[:, u, :], ring[:, u, :], start=True, stop=True
                                          ).then_inc(summed, 1)
                            else:
                                pe.matmul(slot(u, D), ring[:, u, 0:D], onehot[:, u, :], start=True, stop=True
                                          ).then_inc(summed, 1)
                pe.wait_ge(added, STEPS * (turn + 1))

            edge_sums(0)
            pe.wait_ge(w_loaded, WL)
            for q in range(2):
                for j in range(4):
                    ins = pe.transpose(PS[:, 2 + q, j * P:(j + 1) * P], w_raw[:, 4 * q + j, :], ident[:, :])
                ins.then_inc(w_turned, 1)
            pe.wait_ge(wT_ready, 2)
            turn_rows(3)
            pe.wait_ge(rows_stored, 4)
            pe.wait_ge(places_scaled, 1)
            pe.wait_ge(ln_relu, NLN * 2)

            GI = RING // Q

            def spread_group(i, q):
                pe.wait_ge(rows3_loaded[q], i * 16 + 16)
                if not (isinstance(i, int) and i == 0 and q == 0):
                    pe.wait_ge(same_raw, i * GI + q)
                r3 = rows3[:, q * Q:(q + 1) * Q, :].rearrange("a s e -> a (s e)")
                pe.matmul(PS[:, 0, :], pick[:, 0, :], r3, start=True, stop=True)
                pe.matmul(PS[:, 1, :], pick[:, 1, :], r3, start=True, stop=True).then_inc(spread, 1)

            def pick_rows(i, q, at):
                pe.wait_ge(picks_ready, i * GI + (q + 1))
                for s in range(Q):
                    ins = pe.matmul(PS[:, 2 + q % 2, s * P:(s + 1) * P], dstT[:, (q % 2) * Q + s, :],
                                    h_flat[:, bass.ds(at[q * Q + s], D)], start=True, stop=True)
                ins.then_inc(rows_picked, 1)

            def sum_equals(i, q):
                pe.wait_ge(rows_weighted, i * GI + (q + 1))
                pe.wait_ge(same_ready, i * GI + (q + 1))
                if not (isinstance(i, int) and i == 0 and q < 2):
                    pe.wait_ge(sums_taken, i * GI + (q - 1))
                for s in range(Q):
                    ins = pe.matmul(PS[:, 4 + 2 * (q % 2) + s // 2, (s % 2) * 256:(s % 2) * 256 + MROW],
                                    same[:, (q % 2) * Q + s, :], picked[:, (q % 2) * Q + s, :], start=True, stop=True)
                ins.then_inc(equals_summed, 1)

            def back_round(i, first, last):
                for q in range(GI):
                    if q == 0:
                        _, at = nc.values_load_multi_w_load_instructions(
                            off_row[0:1, bass.ds(i * RING, RING)], engines=[mybir.EngineType.PE], min_val=0,
                            max_val=(BLOCKS - 1) * D,
                            skip_runtime_bounds_check_because="the blocks are clamped where the offsets are made")
                    pick_rows(i, q, at)
                    if q or not first:
                        sum_equals(i if q else i - 1, (q - 1) % GI)
                    if q < GI - 1 or not last:
                        spread_group(i if q < GI - 1 else i + 1, (q + 1) % GI)

            spread_group(0, 0)
            back_round(0, True, False)
            with pe.Fori(1, ITERS - 1) as i:
                back_round(i, False, False)
            back_round(ITERS - 1, False, True)
            sum_equals(ITERS - 1, GI - 1)
            pe.wait_ge(degree_ready, 1)
            pe.matmul(PS[:, 0, 0:BLOCKS], tri[:, :], degree[:, :], start=True, stop=True)
            pe.matmul(PS[:, 1, 0:BLOCKS], ones[:, :], degree[:, :], start=True, stop=True).then_inc(nodes_summed, 1)
            pe.wait_ge(sums_taken, STEPS // Q)
            pe.matmul(PS[:, 4, 0:HA], wT[:, 7, :], att_cols[:, :], start=True, stop=True).then_inc(att_folded, 1)
            pe.wait_ge(nodes_counted, 1)
            pe.wait_ge(w3_ready, 1)
            turn_h(1)

            def turn_means(g):
                pe.wait_ge(mean_ready, g + 1)
                if g >= 2:
                    pe.wait_ge(mean_stored, g - 1)
                for j, b in enumerate(range(g * LNG, min(BLOCKS, (g + 1) * LNG))):
                    ins = pe.transpose(PS[:, 2 * (g % 2) + j // 4, (j % 4) * P:(j % 4 + 1) * P], acc_m[:, b, 0:D], ident[:, :])
                ins.then_inc(mean_turned, 1)

            def through_weights(g):
                pe.wait_ge(mean_stored, g + 1)
                if g >= 2:
                    pe.wait_ge(mean_added, g - 1)
                for j, b in enumerate(range(g * LNG, min(BLOCKS, (g + 1) * LNG))):
                    to = PS[:, 4 + 2 * (g % 2) + j // 4, (j % 4) * P:(j % 4 + 1) * P]
                    pe.matmul(to, hT[:, b * P:(b + 1) * P], w_mean[:, 0, :], start=True, stop=False)
                    ins = pe.matmul(to, meanT[:, g % 2, j * P:(j + 1) * P], w_mean[:, 1, :], start=False, stop=True)
                ins.then_inc(mean_summed, 1)

            for g in range(NLN):
                turn_means(g)
                through_weights(g)
            pe.wait_ge(mean_added, NLN)
            turn_h(2)
            edge_sums(1)
            for q in range(ceil_div(BLOCKS, 4)):
                if q >= 8:
                    pe.wait_ge(types_stored, q - 7)
                k = min(4, BLOCKS - 4 * q)
                for j in range(k):
                    ins = pe.transpose(PS[0:TYPES, q % 8, j * P:(j + 1) * P], types_at[:, 4 * q + j, :], ident[:, :])
                ins.then_inc(types_turned, 1)
            pe.wait_ge(types_stored, ceil_div(BLOCKS, 4))
            for q in range(ceil_div(NPAD, 512)):
                w = min(512, NPAD - 512 * q)
                if q >= 2:
                    pe.wait_ge(msg_stored, q - 1)
                pe.matmul(PS[:, q % 2, 0:w], wT[:, 0, :], acc_d[:, q * 512:q * 512 + w], start=True, stop=False)
                pe.matmul(PS[:, q % 2, 0:w], emb_b[:, :], typesT[:, q * 512:q * 512 + w], start=False, stop=True
                          ).then_inc(msg_summed, 1)
            pe.wait_ge(msg_stored, ceil_div(NPAD, 512))

            def turn_gru(q):
                k = min(QW, NPAD - QW * q) // P
                pe.wait_ge(gru_ready, q + 1)
                if q >= 2:
                    pe.wait_ge(gru_added, q - 1)
                for j in range(k):
                    ins = pe.transpose(PS[:, q % 2, j * P:(j + 1) * P], gate[:, q % 2, 3, j * P:(j + 1) * P], ident[:, :])
                ins.then_inc(gru_turned, 1)

            for q in range(NQ):
                w = min(QW, NPAD - QW * q)
                pr = 2 + 2 * (q % 2)
                if q >= 2:
                    pe.wait_ge(rz_ready, 2 * (q - 1))
                    pe.wait_ge(n_summed, q - 1)
                m, hh = msg[:, q * QW:q * QW + w], hT[:, q * QW:q * QW + w]
                for g in range(2):
                    pe.matmul(PS[:, pr, g * QW:g * QW + w], wT[:, 1 + g, :], m, start=True, stop=False)
                    pe.matmul(PS[:, pr, g * QW:g * QW + w], wT[:, 4 + g, :], hh, start=False, stop=True)
                pe.matmul(PS[:, pr + 1, 0:w], wT[:, 3, :], m, start=True, stop=True)
                pe.matmul(PS[:, pr + 1, QW:QW + w], wT[:, 6, :], hh, start=True, stop=True).then_inc(gates_summed, 1)
                if q >= 1:
                    turn_gru(q - 1)
            turn_gru(NQ - 1)
            pe.wait_ge(gru_added, NQ)
            turn_h(3)
            for q in range(ceil_div(BLOCKS, 3)):
                k = min(3, BLOCKS - 3 * q)
                if q >= 8:
                    pe.wait_ge(att_stored, q - 7)
                for j in range(k):
                    b = 3 * q + j
                    ins = pe.matmul(PS[:, q % 8, j * ROW3:(j + 1) * ROW3], hT[:, b * P:(b + 1) * P], w3[:, :],
                                    start=True, stop=True)
                ins.then_inc(att_summed, 1)
            pe.wait_ge(att_stored, NATT)

            def spread_low(i, g):
                pe.wait_ge(lows_loaded[(g // 2) % 2], i * (16 * GROUPS3 // 4) + 16 * (g // 4 + 1))
                if not (isinstance(i, int) and i == 0 and g < 4):
                    pe.wait_ge(low_apart, i * GROUPS3 + (g - 3))
                pe.matmul(PS[:, spread_bank[g % 4], :], ones_row,
                          lows[:, (g // 2) % 2, (g % 2) * G3:(g % 2 + 1) * G3, :].rearrange("p s e -> p (s e)"),
                          start=True, stop=True).then_inc(low_spread, 1)

            def pick_logits(i, g):
                for v in range(2):
                    pe.wait_ge(low_hot[v], i * GROUPS3 + (g + 1))
                if not (isinstance(i, int) and i == 0 and g < 4):
                    pe.wait_ge(multiplied3, i * (GROUPS3 // 2) + (g // 2 - 1))
                for s in range(G3):
                    for v in range(2):
                        for a in range(3):
                            ins = pe.matmul(PS[:, 2 + g % 4, s * P:s * P + HM], low_hots[v][:, g % 4, s * P:(s + 1) * P],
                                            parts3[:, a, v, :], start=(v == 0 and a == 0), stop=(v == 1 and a == 2))
                ins.then_inc(picked3, 1)

            AHEAD3 = 3

            def pick_round(i, last):
                for g in range(GROUPS3):
                    if g + AHEAD3 < GROUPS3 or not last:
                        spread_low(i, g + AHEAD3)
                    pick_logits(i, g)

            pe.wait_ge(parts3_ready, 1)
            for g in range(AHEAD3):
                spread_low(0, g)
            pick_round(0, False)
            with pe.Fori(1, IT3 - 1) as i:
                pick_round(i, False)
            pick_round(IT3 - 1, True)
            pe.wait_ge(ends_turn, 1)
            pe.transpose(PS[0:HEADS, 0, 0:P], row_ends[:, 0:HEADS], ident[:, :])
            pe.transpose(PS[0:HEADS, 0, P:2 * P], row_ends[:, HEADS:2 * HEADS], ident[:, :]).then_inc(turned3, 1)
            pe.wait_ge(carry_row, 1)
            pe.transpose(PS[:, 1, 0:HEADS], rowT[:, 2, :], ident[0:HEADS, 0:HEADS]).then_inc(turned3, 1)
            pe.wait_ge(ends_turn, 2)
            pe.transpose(PS[0:HEADS, 2, 0:P], row_ends[:, 2 * HEADS:3 * HEADS], ident[:, :]).then_inc(turned3, 1)
            pe.wait_ge(carry_row, 2)
            pe.transpose(PS[:, 3, 0:HEADS], rowT[:, 7, :], ident[0:HEADS, 0:HEADS]).then_inc(turned3, 1)

        @block.vector
        def _(dve):
            steps_of_dve = [0]

            def link(ins):
                steps_of_dve[0] += 1
                ins.then_inc(dve_done, 1)
                dve.wait_ge(dve_done, steps_of_dve[0])

            dve.wait_ge(consts_set, 2)
            dve.memset(flat_ring[:, 0:KW], 0.0).then_inc(ring_cleared, 1)
            dve.memset(ones[:, :], 1.0)
            dve.tensor_scalar(minus_p[:, :], pidx[:, :], -1.0, None, ALU.mult)
            dve.memset(one13[:, :], 1.0)
            dve.memset(vw[:, :, :], 1.0)
            dve.tensor_scalar(ident[:, :], iota_k[:, 0:P], pidx[:, 0:1], None, ALU.is_equal)
            dve.tensor_scalar(tri[:, :], iota_k[:, 0:P], pidx[:, 0:1], None, ALU.is_ge)
            link(dve.tensor_scalar(pad_start[:, :], pidx[:, :], float(CREST), 1.0e6, ALU.is_ge, ALU.mult))
            dve.wait_ge(ends_loaded, 128)
            dve.tensor_scalar(dump[:, :], pidx[:, :], float(NPAD), None, ALU.add)
            dve.tensor_scalar(pick[:, 0, :], ones[0:3, :], pidx[0:3, 0:1], 2.0, ALU.mult, ALU.is_equal)
            dve.tensor_scalar(pick[:, 1, :], ones[0:3, :], pidx[0:3, 0:1], 2.0, ALU.mult, ALU.is_lt)
            shift = P.bit_length() - 1
            dve.tensor_scalar(fb_i[:, :], first_dst[:, :], shift, None, ALU.arith_shift_right)
            link(dve.tensor_scalar(pb_i[:, :], prev_dst[:, :], shift, None, ALU.arith_shift_right))
            dve.tensor_copy(fb[:, :], fb_i[:, :])
            link(dve.tensor_copy(pb[:, :], pb_i[:, :]))
            link(dve.scalar_tensor_tensor(out=adv[:, :], in0=fb[:, :], scalar=-1.0, in1=pb[:, :], op0=ALU.add, op1=ALU.subtract))
            dve.tensor_copy(vw[:, :, 1], adv[:, :])
            link(dve.tensor_tensor_scan(adv_sum[:, :], one13[:, 0:CT], adv[:, :], 0.0, ALU.mult, ALU.add))
            dve.tensor_tensor(adv_sum[:, :], adv_sum[:, :], adv[:, :], ALU.subtract).then_inc(adv_ready, 1)
            dve.wait_ge(adv_ready, 1)
            dve.tensor_copy(vw_before[:, :, 1], adv_sum[:, :])
            for t in range(CT):
                dve.memset(vw_before[:, t, 0:1], float(t))
            dve.wait_ge(src3_loaded, 32)
            link(dve.tensor_scalar(low_i, raw3, LOWS - 1, None, ALU.bitwise_and))
            dve.tensor_copy(flat_ring[:, 0:KW], low_i).then_inc(low_made, 1)
            dve.wait_ge(adv_summed, 1)
            link(dve.tensor_tensor(start_step[:, :], fb[:, :], PS[:, 0, 0:CT], ALU.subtract))
            link(dve.tensor_tensor(start_step[:, CT - 1:CT], start_step[:, CT - 1:CT], pad_start[:, :], ALU.add))
            dve.memset(ones_bf, 1.0)
            for t in range(CT):
                w = min(2 * P, KW - t * P)
                ins = dve.tensor_scalar(marks[:, t, 0:w], iota_k[:, t * P:t * P + w], start_step[:, t:t + 1], None, ALU.is_ge)
            ins.then_inc(steps_marked, 1)
            dve.wait_ge(steps_summed, 1)
            pairs = PS[:, 1, 0:2 * KT].rearrange("p (k a) -> p k a", a=2)
            dve.tensor_scalar(chunk_idx[:, :], pairs[:, :, 0], -1.0, None, ALU.add).then_inc(chunks_known, 1)
            link(dve.tensor_tensor(blk[:, :], pairs[:, :, 1], kcol[:, :], ALU.add))
            dve.tensor_scalar(neg_base[:, :], blk[:, :], -float(P), None, ALU.mult)
            link(dve.tensor_tensor(brow[:, :], PS[0:1, 2:6, :].rearrange("p a b -> p (a b)")[:, 0:KW], iota_k[0:1, :], ALU.add))
            link(dve.tensor_scalar(brow[:, :], brow[:, :], float(BLOCKS - 1), 0.0, ALU.min, ALU.max))
            dve.tensor_scalar(off_row[:, :], brow[:, :], float(ROW), None, ALU.mult).then_inc(chunks_known, 1)
            dve.wait_ge(chunks_known, 2)
            dve.memset(msg, 0.0).then_inc(zeros_ready, 1)

            def moments(n, g):
                b0, b1 = g * LNG, min(BLOCKS, (g + 1) * LNG)
                for b in range(b0, b1):
                    ins = dve.bn_stats(stats[:, b, :], X[:, b, :])
                link(ins)
                for b in range(b0, b1):
                    ins = dve.bn_aggr(mv[:, b, :], stats[:, b, :])
                link(ins)
                if g == 0 and n:
                    dve.wait_ge(ln_relu, NLN * n)
                dve.tensor_scalar(ve[:, b0:b1], mv[:, b0:b1, 1], EPS, None, ALU.add).then_inc(ln_var, 1)

            def scales(n, g):
                b0, b1 = g * LNG, min(BLOCKS, (g + 1) * LNG)
                dve.wait_ge(ln_sd, NLN * n + g + 1)
                link(dve.reciprocal(rstd[:, b0:b1], sd[:, b0:b1]))
                dve.scalar_tensor_tensor(out=nmr[:, b0:b1], in0=mv[:, b0:b1, 0], scalar=-1.0,
                                         in1=rstd[:, b0:b1], op0=ALU.mult, op1=ALU.mult).then_inc(ln_scale, 1)

            def layer_norm(n, update=None):
                for g in range(NLN):
                    if update:
                        link(update(slice(g * LNG, min(BLOCKS, (g + 1) * LNG))))
                    moments(n, g)
                    if g:
                        scales(n, g - 1)
                scales(n, NLN - 1)

            dve.wait_ge(x_loaded, 32)
            layer_norm(0)
            dve.wait_ge(rows_gathered[0], 16 * KT)
            for t in range(KT):
                ins = dve.tensor_scalar(rows[0][:, t * P:(t + 1) * P], rows_i[0][:, t * P:(t + 1) * P], neg_base[:, t:t + 1],
                                        None, ALU.add)
            ins.then_inc(rows_ready[0], 1)
            dve.wait_ge(rows_gathered[2], 16 * KT)
            dve.wait_ge(rows_gathered[1], 16 * KT)
            dve.tensor_scalar(src_high, rows_i[1], -P, None, ALU.bitwise_and)
            link(dve.tensor_scalar(src_low, rows_i[1], P - 1, None, ALU.bitwise_and))
            dve.tensor_copy(rows3_bf[:, 0, :], src_high)
            dve.tensor_copy(rows3_bf[:, 1, :], src_low)
            dve.tensor_scalar(rows3_bf[:, 2, :], rows[0], -1.0, OUTSIDE, ALU.max, ALU.min).then_inc(parts_made, 1)
            dve.tensor_scalar(rows[2], rows_i[2], 0.0, float(TYPES - 1), ALU.max, ALU.min).then_inc(rows_ready[2], 1)
            dve.wait_ge(rows_turned, 3)
            link(dve.memset(acc[:, :], 0.0))

            def edge_adds(turn):
                width = (ROW, D)[turn]

                def hots(i, h):
                    k = bass.ds(i * RING + h * HALF, HALF)
                    us = slice(h * HALF, (h + 1) * HALF)
                    lane = iota_k[:, 0:P].unsqueeze(1).broadcast_to([P, HALF, P])
                    rel = dst_rel[:, k].unsqueeze(2).broadcast_to([P, HALF, P])
                    ins = dve.tensor_tensor(onehot[:, us, :], lane, rel, ALU.is_equal)
                    if turn == 0:
                        kinds = iota_k[:, 0:TYPES].unsqueeze(1).broadcast_to([P, HALF, TYPES])
                        kind = type_step[:, k].unsqueeze(2).broadcast_to([P, HALF, TYPES])
                        ins = dve.tensor_tensor(ring[:, us, D:ROW], kinds, kind, ALU.is_equal)
                    ins.then_inc(hot_ready, 1)

                def adds(i, h, at):
                    for s in range(HALF):
                        u = h * HALF + s
                        if u % 2 == 0:
                            dve.wait_ge(summed, i * RING + (STEPS * turn + u + 2))
                        if turn or u or not (isinstance(i, int) and i == 0):
                            dve.wait_ge(added, i * RING + (STEPS * turn + u))
                        a = acc[:, bass.ds(at[u], width)]
                        dve.tensor_tensor(a, a, slot(u, width), ALU.add).then_inc(added, 1)

                def body(i, more):
                    _, at = nc.values_load_multi_w_load_instructions(
                        off_row[0:1, bass.ds(i * RING, RING)], engines=[DVE_ENGINE], min_val=0,
                        max_val=(BLOCKS - 1) * width,
                        skip_runtime_bounds_check_because="the blocks are clamped where the offsets are made")
                    hots(i, 1)
                    adds(i, 0, at)
                    if more:
                        hots(i + 1, 0)
                    adds(i, 1, at)

                hots(0, 0)
                body(0, True)
                with dve.Fori(1, ITERS - 1) as i:
                    body(i, True)
                body(ITERS - 1, False)
                dve.wait_ge(added, STEPS * (turn + 1))

            dve.wait_ge(rows_stored, 3)
            dve.wait_ge(low_turned, 1)
            dve.wait_ge(low_stored, 16)
            edge_adds(0)

            dve.tensor_scalar(off_row[:, :], brow[:, :], float(D), None, ALU.mult).then_inc(places_scaled, 1)
            acc_r = acc[:, :].rearrange("p (b r) -> p b r", r=ROW)
            layer_norm(1, lambda bs: dve.tensor_tensor(X[:, bs, :], X[:, bs, :], acc_r[:, bs, 0:D], ALU.add))
            link(dve.tensor_scalar(in_block[:, :], dst_rel[:, :], float(P), None, ALU.is_lt))
            link(dve.scalar_tensor_tensor(out=in_block[:, :], in0=dst_rel[:, :], scalar=0.0, in1=in_block[:, :],
                                          op0=ALU.is_ge, op1=ALU.mult))
            GI = RING // Q

            def mark(i, q):
                gs = slice((q % 2) * Q, (q % 2 + 1) * Q)
                k = bass.ds(i * RING + q * Q, Q)
                done = i * GI + (q + 1)
                dve.wait_ge(spread, done)
                on_all = [PS[:, bank, :].rearrange("p (s e) -> p s e", s=Q) for bank in range(2)]
                dve.tensor_scalar(dstT[:, gs, :], on_all[0], pidx[:, 0:1], None, ALU.is_equal).then_inc(picks_ready, 1)
                dve.tensor_tensor(same[:, gs, :], on_all[1], src_idx[:, k].unsqueeze(2).broadcast_to([P, Q, P]), ALU.is_equal
                                  ).then_inc(same_raw, 1)
                dve.tensor_scalar(src_less[:, q * Q:(q + 1) * Q], src_idx[:, k], dump[:, 0:1], None, ALU.subtract
                                  ).then_inc(less_ready, 1)
                dve.wait_ge(same_raw, done)
                dve.tensor_tensor(same[:, gs, :], same[:, gs, :], tri[:, :].unsqueeze(1).broadcast_to([P, Q, P]), ALU.mult
                                  ).then_inc(same_ready, 1)
                dve.wait_ge(same_ready, done)
                dve.tensor_reduce(equals[:, q * Q:(q + 1) * Q], same[:, gs, :], AX, ALU.add).then_inc(equals_ready, 1)
                dve.wait_ge(equals_ready, done)
                dve.wait_ge(less_ready, done)
                dve.scalar_tensor_tensor(out=last_src[:, q * Q:(q + 1) * Q], in0=equals[:, q * Q:(q + 1) * Q], scalar=1.0,
                                         in1=src_less[:, q * Q:(q + 1) * Q], op0=ALU.is_equal, op1=ALU.mult
                                         ).then_inc(void_marked, 1)
                dve.wait_ge(void_marked, done)
                for s in range(Q):
                    u = q * Q + s
                    if not (isinstance(i, int) and i == 0):
                        dve.wait_ge(scattered[u % COPIES], i * 32 + (16 * (u // COPIES) - 16))
                dve.tensor_scalar(idx_stage[:, q * Q:(q + 1) * Q], last_src[:, q * Q:(q + 1) * Q], dump[:, 0:1], None, ALU.add
                                  ).then_inc(places_ready, 1)

            for q in range(GI):
                mark(0, q)
            with dve.Fori(1, ITERS) as i:
                for q in range(GI):
                    mark(i, q)

            dve.tensor_copy(types_at[:, :, :], acc_r[:, :, D:ROW])
            dve.tensor_reduce(degree[:, :], acc_r[:, :, D:ROW], AX, ALU.add).then_inc(degree_ready, 1)
            dve.tensor_tensor(X[:, :, :], X[:, :, :], b_mean[:, :].unsqueeze(1).broadcast_to([P, BLOCKS, D]), ALU.add
                              ).then_inc(bias_added, 1)
            dve.wait_ge(degree_ready, 1)
            dve.wait_ge(nodes_summed, 1)
            link(dve.tensor_copy(total[:, :], PS[:, 1, 0:BLOCKS]))
            link(dve.tensor_tensor_scan(before[:, :], one13[:, :], total[:, :], 0.0, ALU.mult, ALU.add))
            link(dve.tensor_tensor(before[:, :], before[:, :], total[:, :], ALU.subtract))
            dve.tensor_scalar(empty[:, :], degree[:, :], 0.0, float(NOBODY), ALU.is_equal, ALU.mult)
            link(dve.tensor_tensor(upto[:, :], before[:, :], PS[:, 0, 0:BLOCKS], ALU.add))
            link(dve.tensor_tensor(upto[:, :], upto[:, :], empty[:, :], ALU.add))
            dve.tensor_tensor(begin_i[:, :], upto[:, :], degree[:, :], ALU.subtract)
            dve.tensor_scalar(end_i[:, :], upto[:, :], -1.0, None, ALU.add).then_inc(nodes_counted, 1)
            dve.wait_ge(w_loaded, WL)
            dve.tensor_tensor(emb_b[:, :], emb_b[:, :], emb[:, :], ALU.add)
            dve.tensor_tensor(brz[:, :], bcol[:, 0:2], bcol[:, 3:5], ALU.add)
            dve.wait_ge(att_folded, 1)
            dve.tensor_copy(w3[:, D:ROW3], PS[:, 4, 0:HA]).then_inc(w3_ready, 1)
            dve.wait_ge(bias_added, 1)

            def add_means(g):
                b0, b1 = g * LNG, min(BLOCKS, (g + 1) * LNG)
                dve.wait_ge(mean_summed, g + 1)
                xs = X[:, b0:b1, :].rearrange("p b f -> p (b f)")
                dve.tensor_tensor(xs, xs, PS[:, 4 + 2 * (g % 2):6 + 2 * (g % 2), :].rearrange("p a b -> p (a b)")[:, 0:(b1 - b0) * P],
                                  ALU.add).then_inc(mean_added, 1)
                dve.wait_ge(mean_added, g + 1)
                moments(2, g)

            for g in range(NLN):
                b0, b1 = g * LNG, min(BLOCKS, (g + 1) * LNG)
                for c in range(2 * g, min(2 * g + 2, PIECES)):
                    p0, p1 = c * PIECE, min(BLOCKS, (c + 1) * PIECE)
                    dve.wait_ge(pieces_loaded[c % 2], 16 * COPIES * (c // 2 + 1))
                    dve.tensor_reduce(acc[:, p0 * MROW:p1 * MROW],
                                      pieces[c % 2][:, 0:COPIES * (p1 - p0) * MROW].rearrange("p (n m) -> p m n", n=COPIES),
                                      AX, ALU.add).then_inc(piece_added, 1)
                    if g >= 2 and c == 2 * g:
                        scales(2, g - 2)
                dve.wait_ge(piece_added, min(2 * g + 2, PIECES))
                link(dve.tensor_scalar(rcount[:, b0:b1], acc_m[:, b0:b1, D], 1.0, None, ALU.max))
                dve.reciprocal(rcount[:, b0:b1], rcount[:, b0:b1]).then_inc(counts_ready, 1)
                if g:
                    add_means(g - 1)
            scales(2, NLN - 2)
            add_means(NLN - 1)
            scales(2, NLN - 1)
            link(dve.memset(acc[:, 0:NPAD], 0.0))
            dve.wait_ge(h_stored, 2 * ceil_div(BLOCKS, 4))
            edge_adds(1)

            dve.memset(sumsN[:, :, :], 0.0)
            dve.wait_ge(last_loaded, 80)
            link(dve.tensor_tensor(not_start, dst3, prev3, ALU.is_equal))
            link(dve.memset(not_start[0:1, 0:1], 0.0))
            link(dve.tensor_scalar(start_low, not_start, -1.0, BIG, ALU.add, ALU.mult))
            dve.tensor_reduce(row_ends[:, HEADS:HEADS + 1], start_low, AX, ALU.min)
            link(dve.tensor_scalar(src3[:, 0:ONEHOT_COLS], src3[:, 0:ONEHOT_COLS], shift + 1, None, ALU.arith_shift_right))
            dve.memset(ones_row, 1.0)

            def gru_add(q):
                k = min(QW, NPAD - QW * q) // P
                dve.wait_ge(gru_turned, q + 1)
                dve.tensor_tensor(X[:, 2 * q:2 * q + k, :].rearrange("p b f -> p (b f)"),
                                  X[:, 2 * q:2 * q + k, :].rearrange("p b f -> p (b f)"), PS[:, q % 2, 0:k * P], ALU.add
                                  ).then_inc(gru_added, 1)

            for q in range(NQ):
                w = min(QW, NPAD - QW * q)
                pr = 2 + 2 * (q % 2)
                r, z, n, t = (gate[:, q % 2, a, 0:w] for a in range(4))
                dve.wait_ge(rz_ready, 2 * q + 2)
                if q >= 2:
                    dve.wait_ge(gru_turned, q - 1)
                link(dve.scalar_tensor_tensor(out=t, in0=PS[:, pr + 1, QW:QW + w], scalar=bcol[:, 5:6], in1=r,
                                              op0=ALU.add, op1=ALU.mult))
                dve.tensor_tensor(t, t, PS[:, pr + 1, 0:w], ALU.add).then_inc(n_summed, 1)
                if q >= 1:
                    gru_add(q - 1)
                dve.wait_ge(n_ready, q + 1)
                link(dve.tensor_tensor(t, hT[:, q * QW:q * QW + w], n, ALU.subtract))
                link(dve.tensor_tensor(t, t, z, ALU.mult))
                dve.tensor_tensor(t, t, n, ALU.add).then_inc(gru_ready, 1)
            gru_add(NQ - 1)
            dve.wait_ge(gru_added, NQ)
            layer_norm(3)


            dve.wait_ge(att_stored, NATT)
            link(dve.memset(left3, 0.0))
            for v in range(2):
                count = (BLOCKS - v + 1) // 2
                ins = dve.tensor_copy(left3[:, v, :].rearrange("p (h b) -> p h b", h=HEADS)[:, :, 0:count],
                                      HWv[:, v:BLOCKS:2, D:D + HEADS].rearrange("p b h -> p h b"))
            link(ins)
            link(dve.tensor_copy(parts3[:, 0, :, :], left3))
            link(dve.tensor_tensor(left3, left3, parts3[:, 0, :, :], ALU.subtract))
            link(dve.tensor_copy(parts3[:, 1, :, :], left3))
            link(dve.tensor_tensor(left3, left3, parts3[:, 1, :, :], ALU.subtract))
            dve.tensor_copy(parts3[:, 2, :, :], left3).then_inc(parts3_ready, 1)
            dve.wait_ge(parts3_ready, 1)

            def low_hots_second(i, g):
                dve.wait_ge(low_apart, i * GROUPS3 + (g + 1))
                if not (isinstance(i, int) and i == 0 and g < 4):
                    dve.wait_ge(picked3, i * GROUPS3 + (g - 3))
                dve.tensor_scalar(low_hots[1][:, g % 4, :], apart[:, g % 4, :], float(P), None, ALU.is_equal
                                  ).then_inc(low_hot[1], 1)

            def high_hots3(i, m):
                dve.tensor_tensor(highs[:, m % 2, :, :], iota_k[:, 0:HIGHS].unsqueeze(1).broadcast_to([P, B3, HIGHS]),
                                  src3[:, bass.ds(i * COLS3 + m * B3, B3)].unsqueeze(2).broadcast_to([P, B3, HIGHS]),
                                  ALU.is_equal).then_inc(high_hot, 1)

            def take_logits(i, last):
                M3 = GROUPS3 // 2
                for m in range(M3):
                    more = m < M3 - 1 or not last
                    if more:
                        low_hots_second(i, 2 * m + 2)
                        low_hots_second(i, 2 * m + 3)
                    dve.wait_ge(high_hot, i * M3 + (m + 1))
                    dve.wait_ge(picked3, i * GROUPS3 + (2 * m + 2))
                    dve.tensor_tensor(
                        products[:, m % 2, :, :].rearrange("p s (h b) -> p s h b", h=HEADS),
                        PS[:, 2 + 2 * (m % 2):4 + 2 * (m % 2), :].rearrange("p c (s m) -> p (c s) m", m=P)[:, :, 0:HM].rearrange(
                            "p s (h b) -> p s h b", h=HEADS),
                        highs[:, m % 2, :, :].unsqueeze(2).broadcast_to([P, B3, HEADS, HIGHS]),
                        ALU.mult).then_inc(multiplied3, 1)
                    if more:
                        high_hots3(i, m + 1)
                    dve.wait_ge(multiplied3, i * M3 + (m + 1))
                    dve.tensor_reduce(al3[:, bass.ds(i * COLS3 + m * B3, B3), :],
                                      products[:, m % 2, :, :].rearrange("p s (h b) -> p s h b", h=HEADS), AX, ALU.add
                                      ).then_inc(picked_logits, 1)

            low_hots_second(0, 0)
            low_hots_second(0, 1)
            high_hots3(0, 0)
            take_logits(0, False)
            with dve.Fori(1, IT3 // 2) as i:
                take_logits(i, False)
            dve.wait_ge(first_back, 16)
            dve.wait_ge(filled_back, 16)
            for h in range(HEADS):
                ins = dve.tensor_tensor_scan(aj3[:, :, h], not_start, aj3[:, :, h], first_logits[:, HEADS + h:HEADS + h + 1],
                                             ALU.mult, ALU.add)
            link(ins)
            with dve.Fori(IT3 // 2, IT3 - 1) as i:
                take_logits(i, False)
            take_logits(IT3 - 1, True)
            dve.wait_ge(picked_logits, IT3 * GROUPS3 // 2)
            dve.wait_ge(all_logits, (ROUNDS3 - 1) * 4 + ceil_div(TAIL3, QUARTER))
            a = al[:, 0:AN]
            link(dve.tensor_tensor(a, a, aj, ALU.add))
            link(dve.scalar_tensor_tensor(out=a, in0=a, scalar=0.2, in1=a, op0=ALU.mult, op1=ALU.max))
            for h in range(HEADS):
                ins = dve.tensor_tensor_scan(mx3[:, :, h], start_low, al3[:, 0:CHUNKS, h], -BIG, ALU.add, ALU.max)
            link(ins)
            dve.tensor_copy(row_ends[:, 0:HEADS], mx3[:, CHUNKS - 1, :])
            for h in range(1, HEADS):
                dve.tensor_copy(row_ends[:, HEADS + h:HEADS + h + 1], row_ends[:, HEADS:HEADS + 1])
            dve.tensor_copy(carry[:, 0:1], pidx[:, :]).then_inc(ends_turn, 1)
            dve.wait_ge(turned3, 1)
            link(dve.tensor_copy(rowT[:, 0:2, :].rearrange("p a b -> p (a b)"), PS[0:HEADS, 0, 0:2 * P]))
            dve.memset(rowT[:, 2, 0:1], -BIG)
            link(dve.tensor_tensor_scan(rowT[:, 3, :], rowT[:, 1, :], rowT[:, 0, :], -BIG, ALU.add, ALU.max))
            dve.tensor_copy(rowT[:, 2, 1:P], rowT[:, 3, 0:P - 1]).then_inc(carry_row, 1)
            dve.wait_ge(turned3, 2)
            link(dve.tensor_copy(carry[:, 0:HEADS], PS[:, 1, 0:HEADS]))
            for h in range(HEADS):
                ins = dve.tensor_tensor_scan(mx3[:, :, h], start_low, al3[:, 0:CHUNKS, h], carry[:, h:h + 1], ALU.add, ALU.max)
            link(ins)
            link(dve.tensor_tensor(aj[:, HEADS:AN], mx[:, 0:AN - HEADS], mx[:, HEADS:AN], ALU.subtract))
            link(dve.tensor_tensor(aj[:, 0:HEADS], carry[:, 0:HEADS], mx[:, 0:HEADS], ALU.subtract))
            dve.tensor_tensor(aj3, aj3, start_low.unsqueeze(2).broadcast_to([P, CHUNKS, HEADS]), ALU.add).then_inc(exp_in, 1)
            dve.tensor_tensor(a, a, mx, ALU.subtract).then_inc(exp_in, 1)
            link(dve.tensor_tensor(rowT[:, 5, :], rowT[:, 2, :], rowT[:, 3, :], ALU.subtract))
            dve.tensor_tensor(rowT[:, 5, :], rowT[:, 5, :], rowT[:, 1, :], ALU.add).then_inc(exp_in, 1)
            dve.wait_ge(exp_out, 3)
            for h in range(HEADS):
                ins = dve.tensor_tensor_scan(mx3[:, :, h], aj3[:, :, h], al3[:, 0:CHUNKS, h], 0.0, ALU.mult, ALU.add)
            link(ins)
            dve.tensor_copy(row_ends[:, 2 * HEADS:3 * HEADS], mx3[:, CHUNKS - 1, :]).then_inc(ends_turn, 1)
            dve.wait_ge(turned3, 3)
            link(dve.tensor_copy(rowT[:, 4, :], PS[0:HEADS, 2, 0:P]))
            dve.memset(rowT[:, 7, 0:1], 0.0)
            link(dve.tensor_tensor_scan(rowT[:, 6, :], rowT[:, 5, :], rowT[:, 4, :], 0.0, ALU.mult, ALU.add))
            dve.tensor_copy(rowT[:, 7, 1:P], rowT[:, 6, 0:P - 1]).then_inc(carry_row, 1)
            dve.wait_ge(turned3, 4)
            link(dve.tensor_copy(carry[:, HEADS:2 * HEADS], PS[:, 3, 0:HEADS]))
            for h in range(HEADS):
                ins = dve.tensor_tensor_scan(mx3[:, :, h], aj3[:, :, h], al3[:, 0:CHUNKS, h], carry[:, HEADS + h:HEADS + h + 1],
                                             ALU.mult, ALU.add)
            ins.then_inc(sums_ready, 1)
            for n in range(FINAL):
                bs = slice(n * FB, (n + 1) * FB)
                dve.wait_ge(sums_back[n], 16 * FB)
                link(dve.tensor_scalar(ratio[:, bs, :], sumsN[:, bs, :], 1e-16, None, ALU.add))
                link(dve.reciprocal(ratio[:, bs, :], ratio[:, bs, :]))
                link(dve.tensor_tensor(ratio[:, bs, :], ratio[:, bs, :], sumsN[:, bs, :], ALU.mult))
                values = HWv[:, bs, 0:D].rearrange("p b (h c) -> p b h c", h=HEADS)
                link(dve.tensor_tensor(values, values, ratio[:, bs, :].unsqueeze(3).broadcast_to([P, FB, HEADS, C]), ALU.mult))
                dve.tensor_tensor(X[:, bs, :], X[:, bs, :], HWv[:, bs, 0:D], ALU.add).then_inc(out_ready, 1)


_NAMES = ["x", "src", "dst", "edge_type_9", "edge_weight1", "L1_gnn_W", "L1_gnn_b", "L2_gnn_W_msg", "L2_gnn_b_msg",
          "L2_gnn_edge_embed", "L2_gnn_W_ih", "L2_gnn_W_hh", "L2_gnn_b_ih", "L2_gnn_b_hh", "L3_gnn_weight", "L3_gnn_att"]


def kernel(**inputs):
    import numpy as np
    import concourse.bacc as bacc
    from concourse.bass_utils import run_bass_kernel_spmd as run

    nc = bacc.Bacc("TRN2", target_bir_lowering=False, num_devices=1)
    arrays, args = {}, []
    for name in _NAMES:
        a = np.ascontiguousarray(inputs[name])
        if name == "edge_weight1":
            a = a.reshape(-1)
        arrays[f"in_{name}"] = a
        args.append(nc.dram_tensor(f"in_{name}", a.shape, mybir.dt.from_np(a.dtype), kind="ExternalInput").ap())
    out = nc.dram_tensor("out", inputs["x"].shape, F32, kind="ExternalOutput").ap()
    build(nc, *args, out)
    return run(nc, [arrays], core_ids=[0]).results[0]["out"]
```
